# Optimizing a Trainium2 kernel written in Bass

```python
import numpy as np
import jax
import jax.numpy as jnp

def _softmax(x, axis=-1):
    return jax.nn.softmax(x, axis=axis)

def _gelu(x):
    return jax.nn.gelu(x, approximate=True)

def _silu(x):
    return jax.nn.silu(x)

def _sigmoid(x):
    return jax.nn.sigmoid(x)

def _layernorm(x, axis=-1, eps=1e-05):
    m = jnp.mean(x, axis=axis, keepdims=True)
    v = jnp.var(x, axis=axis, keepdims=True)
    return (x - m) / jnp.sqrt(v + eps)

def _scatter_add(tgt, idx, src, axis=0):
    return tgt.at[idx].add(src)

def _segment_sum(src, seg, n):
    return jax.ops.segment_sum(src, seg, n)
kernel_name = 'mk_adj_resnorm_d1_adj_r2_04494c'

def setup_inputs(seed: int=0):
    np.random.seed(seed)
    _w = jnp.asarray

    def _rec_inputs():
        import jax
        import jax.numpy as jnp
        _gk = jax.random.key(seed)
        x = -0.001003 + 1 * jax.random.normal(jax.random.fold_in(_gk, 1), (4096, 128), jnp.float32)
        _a = jax.random.bernoulli(jax.random.fold_in(_gk, 2), 0.00390625, (4096, 4096))
        adj = _a.astype(jnp.int32)
        return (x, adj)
    x, adj = _rec_inputs()

    def _L0_gnn_setup():
        import jax, jax.numpy as jnp
        import numpy as np
        IN_FEATURES = 128
        OUT_FEATURES = 128
        N_HEADS = 4
        N_HIDDEN = OUT_FEATURES // N_HEADS
        N_NODES = 3072
        SLOPE = 0.01
        MASK_VAL = -9000000000000000.0
        key = jax.random.key(seed)
        k1, k2, k3, k4 = jax.random.split(key, 4)
        h = jax.random.normal(k1, (N_NODES, IN_FEATURES), dtype=jnp.float32)
        adj_mat = jax.random.randint(k2, (N_NODES, N_NODES), 0, 2, dtype=jnp.int32)
        W = jax.random.normal(k3, (IN_FEATURES, N_HIDDEN * N_HEADS), dtype=jnp.float32) * (1.414 * np.sqrt(2.0 / (IN_FEATURES + N_HIDDEN * N_HEADS)))
        a = jax.random.normal(k4, (N_HEADS, 2 * N_HIDDEN, 1), dtype=jnp.float32) * (1.414 * np.sqrt(2.0 / (2 * N_HIDDEN + 1)))
        return {'h': h, 'adj_mat': adj_mat, 'W': W, 'a': a}
    _L0_gnn_all = _L0_gnn_setup()
    _L0_gnn_in = {k: v for k, v in _L0_gnn_all.items() if k in ('W', 'a')}
    del _L0_gnn_all
    return {'x': x, 'adj': adj, 'L0_gnn_W': _L0_gnn_in['W'], 'L0_gnn_a': _L0_gnn_in['a']}

def reference(x, adj, L0_gnn_W, L0_gnn_a):
    import jax
    import jax.numpy as jnp

    def _L0_gnn_ref(h, adj_mat, W, a):
        import jax, jax.numpy as jnp
        import numpy as np
        IN_FEATURES = 128
        OUT_FEATURES = 128
        N_HEADS = 4
        N_HIDDEN = OUT_FEATURES // N_HEADS
        N_NODES = 3072
        SLOPE = 0.01
        MASK_VAL = -9000000000000000.0
        n_nodes = h.shape[0]
        ht = (h @ W).reshape(n_nodes, N_HEADS, N_HIDDEN).transpose(1, 0, 2)
        src = jnp.einsum('hnd,hd->hn', ht, a[:, :N_HIDDEN, 0])
        tgt = jnp.einsum('hnd,hd->hn', ht, a[:, N_HIDDEN:, 0])
        e = src[:, :, None] + tgt[:, None, :]
        e = jnp.where(e >= 0, e, SLOPE * e)
        e = jnp.where(adj_mat[None, :, :] > 0, e, MASK_VAL)
        attn = jax.nn.softmax(e, axis=-1)
        h_prime = jnp.einsum('hnm,hmd->hnd', attn, ht)
        return h_prime.transpose(1, 0, 2).reshape(n_nodes, OUT_FEATURES)
    x = _layernorm(x + _L0_gnn_ref(x, adj, L0_gnn_W, L0_gnn_a), axis=-1)
    return x

_drawn_inputs = setup_inputs


def setup_inputs(seed=0):
    import zlib

    import numpy as np

    out = dict(_drawn_inputs(seed))
    spreads = {}
    factors = {}
    for name, (base, spread) in spreads.items():
        noise = np.random.default_rng([zlib.crc32(name.encode()), seed]).standard_normal(out[name].shape)
        drawn = base * np.exp(spread * noise) if base else spread * noise
        out[name] = jnp.asarray(drawn.astype(out[name].dtype))
    for name, factor in factors.items():
        out[name] = (out[name] * factor).astype(out[name].dtype)
    return out
```

```python
import concourse.bass as bass
from concourse import mybir
from contextlib import ExitStack


def graph_attention_residual_norm(
    nc: bass.Bass,
    x: bass.AP,
    adj: bass.AP,
    W: bass.AP,
    a: bass.AP,
    score_rows: bass.AP,
    out: bass.AP,
):
    fp32 = mybir.dt.float32
    bf16 = mybir.dt.bfloat16
    fp8 = mybir.dt.float8e4
    i32 = mybir.dt.int32
    u32 = mybir.dt.uint32
    u8 = mybir.dt.uint8
    ALU = mybir.AluOpType
    ACT = mybir.ActivationFunctionType
    AX = mybir.AxisListType

    N, F = x.shape
    H = a.shape[0]
    D = F // H
    K = D + 1
    PARTS = 3
    KP = PARTS * K
    P = 128
    R = 4
    B = N // (P * R)
    T = B * R
    CH = 1024
    NCH = N // CH
    NT = CH // P
    HB = B // 2
    HALF = N // 2
    STEPS = 2 * NT
    GROUPS = H * B
    ALLG = NCH * GROUPS
    ACC = 6
    PER = 2
    NB_ACC = NT // PER
    BIG = float(2 ** 60)
    TINY = float(2.0 ** -100)
    CSLOTS, ISLOTS, JSLOTS = 3, 2, 2
    EVAC_AT = 1
    ROW_AT = (5, 9, 13)
    X_AT = 18
    CONVERT_AT = [i * (GROUPS - 5) // (STEPS - 1) for i in range(STEPS)]
    TURN_AT = [at + 1 for at in CONVERT_AT]
    STORE_AT = [at + 3 for at in CONVERT_AT]
    NOEDGE, EDGE_BITS, I_SHIFT = 0xB6, 0x90, 4
    word = lambda byte: byte * 0x01010101

    def dve_tiles(g):
        return (1, 1, 1, 1)[g % 4]

    def j_by_matmul(g):
        return g % 2 == 1

    act_before = [0]
    dve_before = [0]
    j_before = [0]
    for g in range(ALLG):
        act_before.append(act_before[-1] + R - dve_tiles(g))
        dve_before.append(dve_before[-1] + dve_tiles(g))
        j_before.append(j_before[-1] + (not j_by_matmul(g)))

    def bank_of(s, j):
        return ((s % H) * NB_ACC + j) % ACC

    def evacuations_before(s, j):
        had = [(s0, j0) for s0 in range(s) for j0 in range(NB_ACC) if bank_of(s0, j0) == bank_of(s, j)]
        return had[-1][0] * NB_ACC + had[-1][1] + 1 if had else None

    ctx = ExitStack()
    with ctx:
        def sb(name, shape, dt):
            return ctx.enter_context(nc.sbuf_tensor(name, shape, dt))

        def pb(name, shape, dt):
            return ctx.enter_context(nc.psum_tensor(name, shape, dt))

        def sem(name):
            return ctx.enter_context(nc.semaphore(name))

        adj_rows = sb("adj_rows", [P, 2, HALF], i32)
        edge_rows = sb("edge_rows", [P, 2, HALF], fp8)
        edges = sb("edges", [P, 2, B, CH * R], u8)
        above = sb("above", [P, CSLOTS, CH * R], u8)
        imat = sb("imat", [P, ISLOTS, CH * R], u8)
        jmat = sb("jmat", [P, JSLOTS, CH * R], u8)
        weights = sb("weights", [P, T + 1, H, 2 * KP], bf16)
        srow = sb("srow", [P, 2, CH], fp32)
        sums_buf = sb("sums_buf", [P, 2 * NT * 2 * KP + NT * H * K], fp32)
        sums = sums_buf[:, 0:2 * NT * 2 * KP].rearrange("p (e j c) -> p e j c", e=2, j=NT)
        heads = sums_buf[:, 2 * NT * 2 * KP:].rearrange("p (j h k) -> p j h k", j=NT, h=H)
        joined = sb("joined", [P, NT, 2, K], fp32)
        rows_buf = sb("rows_buf", [P, 2, NT, F], fp32)
        xres, y = rows_buf[:, 0, :, :], rows_buf[:, 1, :, :]
        rden = sb("rden", [P, NT, H], fp32)
        mean = sb("mean", [P, NT], fp32)
        var = sb("var", [P, NT], fp32)
        rstd = sb("rstd", [P, NT], fp32)
        power = sb("power", [P, NT], fp32)
        ident = sb("ident", [P, P], fp32)
        ones = sb("ones", [P, P], bf16)
        onesf = sb("onesf", [H, P], fp32)
        wraw = sb("wraw", [P, F], fp32)
        avec = sb("avec", [P, H, 2, D], fp32)
        wa = sb("wa", [P, 2, H], fp32)
        wx = sb("wx", [P, H, K], fp32)
        sT = sb("sT", [P, N // P, H], fp32)
        t = sb("t", [P, T, H], fp32)
        tneg = sb("tneg", [P, T, H], fp32)
        tbig = sb("tbig", [P, T, H], fp32)
        trel = sb("trel", [P, T, H], fp32)
        eA = sb("eA", [P, T, H], fp32)
        eB = sb("eB", [P, T, H], fp32)
        ab = sb("ab", [P, N // P, H, 2], fp32)
        tmax = sb("tmax", [P, H], fp32)
        tcol = sb("tcol", [H, 1], fp32)
        tdiag = sb("tdiag", [H, H], fp32)
        tall = sb("tall", [P, H], fp32)
        meanw = sb("meanw", [P, H, K], fp32)

        early = edges[:, 1, :, :].rearrange("p b c -> p (b c)").bitcast(fp32)
        xq = early[:, 0:T * F].rearrange("p (b r f) -> p b r f", b=B, r=R)
        xT = early[:, T * F:2 * T * F]
        s4 = early[0:H, 0:N]
        h1 = sums_buf[:, :].rearrange("p (t h k) -> p t h k", t=T, h=H)
        jm = jmat[:, :, :].rearrange("p s c -> p (s c)").bitcast(fp32)
        wprod = jm[:, 0:2 * F].rearrange("p (h k d) -> p h k d", h=H, k=2)
        MORE = (T + 1) * K
        split_a = rows_buf[:, :, :, :].rearrange("p z j f -> p (z j f)")[:, 0:MORE]
        split_b = jm[:, 0:MORE]

        acc = [pb(f"acc{i}", [P, PER, 2, KP], fp32) for i in range(ACC)]
        tr = [pb(f"tr{i}", [P, 512], fp32) for i in range(2)]

        def proj_bank(p):
            return acc[p % ACC][:, :, :, :].rearrange("p j z c -> p (j z c)")[:, 0:2 * H * K]

        x_in, w_in, a_in, xres_in = sem("x_in"), sem("w_in"), sem("a_in"), sem("xres_in")
        adj_in = [sem(f"adj_in{i}") for i in range(2)]
        srow_in = [sem(f"srow_in{i}") for i in range(2)]
        s4_out, y_out = sem("s4_out"), sem("y_out")
        consts = sem("consts")
        wx_ready = sem("wx_ready")
        tr_filled = sem("tr_filled")
        tr_read = sem("tr_read")
        proj_done, proj_read = sem("proj_done"), sem("proj_read")
        dve_chain = sem("dve_chain")
        pool_chain = sem("pool_chain")
        t_ready = sem("t_ready")
        tmax_ready, tdiag_ready = sem("tmax_ready"), sem("tdiag_ready")
        exp_in, exp_done = sem("exp_in"), sem("exp_done")
        exps_free = sem("exps_free")
        a_split, b_split = sem("a_split"), sem("b_split")
        mean_ready = sem("mean_ready")
        rows_converted = sem("rows_converted")
        words_turned = sem("words_turned")
        edges_ready = sem("edges_ready")
        act_above, dve_above = sem("act_above"), sem("dve_above")
        i_ready, j_ready = sem("i_ready"), sem("j_ready")
        group_summed = sem("group_summed")
        bank_read = sem("bank_read")
        combined = sem("combined")
        rden_ready, y_ready, mean_done = sem("rden_ready"), sem("y_ready"), sem("mean_done")
        sq_ready, var_done, y_normed = sem("sq_ready"), sem("var_done"), sem("y_normed")

        block = ctx.enter_context(nc.Block())

        XT_BANKS = B
        S4_BANKS = N // 512
        ST_BANK = XT_BANKS + S4_BANKS

        x_tiles = x.rearrange("(b q r) f -> q b (r f)", q=P, r=R)
        x_rows = x.rearrange("(c j p) f -> c p j f", p=P, j=NT)
        out_rows = out.rearrange("(c j p) f -> c p j f", p=P, j=NT)

        @block.sync
        def _(sp):
            sp.dma_start(xq.rearrange("p b r f -> p b (r f)"), x_tiles).then_inc(x_in, 16)
            sp.dma_start(wraw[:, :], W).then_inc(w_in, 16)
            sp.dma_start(avec[:, :, :, :].rearrange("p h k d -> p (h k d)"),
                         a.rearrange("h e o -> (h e o)").partition_broadcast(P)).then_inc(a_in, 16)

            def load_adj(k):
                if k >= 2:
                    sp.wait_ge(rows_converted, k - 1)
                n, half = k // 2, k % 2
                sp.dma_start(adj_rows[:, k % 2, :],
                             adj[n * P:(n + 1) * P, half * HALF:(half + 1) * HALF]).then_inc(adj_in[k % 2], 16)

            def load_srow(s):
                c, h = s // H, s % H
                if s >= 2:
                    sp.wait_ge(act_above, act_before[(s - 1) * B])
                    sp.wait_ge(dve_above, dve_before[(s - 1) * B])
                sp.dma_start(srow[:, s % 2, :],
                             score_rows[h, c * CH:(c + 1) * CH].partition_broadcast(P)).then_inc(srow_in[s % 2], 16)

            for k in range(2):
                load_adj(k)
            sp.wait_ge(tr_read, ST_BANK)
            sp.dma_start(score_rows, s4).then_inc(s4_out, 16)
            sp.wait_ge(s4_out, 16)
            load_srow(0)
            load_srow(1)
            for k in range(2, STEPS):
                load_adj(k)
            load_adj(STEPS)
            load_adj(STEPS + 1)
            for g in range(ALLG):
                c, gc, s = g // GROUPS, g % GROUPS, g // B
                if gc == X_AT:
                    if c:
                        sp.wait_ge(var_done, c)
                    else:
                        sp.wait_ge(a_split, H)
                    sp.dma_start(xres, x_rows[c]).then_inc(xres_in, 16)
                if g % B == 0 and s >= 1 and s + 1 < NCH * H:
                    load_srow(s + 1)
                for i in range(STEPS):
                    k = (c + 1) * STEPS + i + 2
                    if CONVERT_AT[i] == gc and k < NCH * STEPS:
                        load_adj(k)
                if gc == X_AT and c:
                    sp.wait_ge(y_normed, c)
                    sp.dma_start(out_rows[c - 1], y).then_inc(y_out, 16)
            sp.wait_ge(y_normed, NCH)
            sp.dma_start(out_rows[NCH - 1], y).then_inc(y_out, 16)
            sp.wait_ge(y_out, 16 * NCH)

        @block.gpsimd
        def _(pool):
            made = [0]

            def link(ins):
                made[0] += 1
                ins.then_inc(pool_chain, 1)
                pool.wait_ge(pool_chain, made[0])

            link(pool.memset(ident[:, :], 0.0))
            link(pool.affine_select(out=ident[:, :], in_=ident[:, :], compare_op=ALU.not_equal, fill=1.0,
                                    base=0, pattern=[[-1, P]], channel_multiplier=1))
            link(pool.memset(ones[:, :], 1.0))
            link(pool.memset(power[:, :], -0.5))
            pool.memset(onesf[:, :], 1.0).then_inc(consts, 1)

            fb = split_b.rearrange("p (t k) -> p t k", k=K)
            pool.wait_ge(mean_ready, 1)
            pool.wait_ge(exp_done, 2)
            for h in range(H):
                w = weights[:, :, h, KP:2 * KP].rearrange("p t (c k) -> p t c k", k=K)
                if h:
                    pool.wait_ge(b_split, h)
                link(pool.tensor_tensor(fb[:, 0:T, :], h1[:, :, h, :],
                                        eB[:, :, h:h + 1].broadcast_to([P, T, K]), ALU.mult))
                link(pool.tensor_scalar(fb[:, 0:T, :], fb[:, 0:T, :], -1.0, None, ALU.mult))
                link(pool.tensor_copy(fb[:, T, :], meanw[:, h, :]))
                link(pool.tensor_copy(w[:, :, 0, :], fb))
                link(pool.tensor_tensor(fb, fb, w[:, :, 0, :], ALU.subtract))
                link(pool.tensor_copy(w[:, :, 1, :], fb))
                link(pool.tensor_tensor(fb, fb, w[:, :, 1, :], ALU.subtract))
                pool.tensor_copy(w[:, :, 2, :], fb).then_inc(b_split, 1)

            def combine(s):
                c, h = s // H, s % H
                pool.wait_ge(bank_read, NB_ACC * (s + 1))
                if s:
                    pool.wait_ge(combined, s)
                e = sums[:, s % 2, :, :].rearrange("p j (z c k) -> p (j z) c k", z=2, k=K)
                both = joined[:, :, :, :].rearrange("p j z k -> p (j z) k")
                link(pool.tensor_tensor(both, e[:, :, 0, :], e[:, :, 1, :], ALU.add))
                link(pool.tensor_tensor(both, both, e[:, :, 2, :], ALU.add))
                rows = ab[:, c * NT:(c + 1) * NT, h, :]
                for z in range(2):
                    last = pool.tensor_tensor(joined[:, :, z, :], joined[:, :, z, :],
                                              rows[:, :, z:z + 1].broadcast_to([P, NT, K]), ALU.mult)
                link(last)
                pool.tensor_tensor(heads[:, :, h, :], joined[:, :, 0, :], joined[:, :, 1, :],
                                   ALU.add).then_inc(combined, 1)

            def finish(c):
                pool.wait_ge(rden_ready, c + 1)
                if c:
                    pool.wait_ge(y_out, 16 * c)
                for h in range(H):
                    last = pool.tensor_tensor(y[:, :, h * D:(h + 1) * D], heads[:, :, h, 0:D],
                                              rden[:, :, h:h + 1].broadcast_to([P, NT, D]), ALU.mult)
                link(last)
                pool.wait_ge(xres_in, 16 * (c + 1))
                pool.tensor_tensor(y[:, :, :], y[:, :, :], xres[:, :, :], ALU.add).then_inc(y_ready, 1)
                pool.wait_ge(mean_done, c + 1)
                link(pool.tensor_tensor(y[:, :, :], y[:, :, :],
                                        mean[:, :].unsqueeze(2).broadcast_to([P, NT, F]), ALU.subtract))
                pool.tensor_tensor(xres[:, :, :], y[:, :, :], y[:, :, :], ALU.mult).then_inc(sq_ready, 1)
                pool.wait_ge(var_done, c + 1)
                link(pool.tensor_scalar(rstd[:, :], var[:, :], 1.0 / F, 1e-5, ALU.mult, ALU.add))
                link(pool.tensor_tensor(rstd[:, :], rstd[:, :], power[:, :], ALU.pow))
                pool.tensor_tensor(y[:, :, :], y[:, :, :],
                                   rstd[:, :].unsqueeze(2).broadcast_to([P, NT, F]),
                                   ALU.mult).then_inc(y_normed, 1)

            for c in range(NCH):
                for h in range(H):
                    combine(c * H + h)
                finish(c)

        @block.scalar
        def _(act):
            for k in range(XT_BANKS):
                act.wait_ge(tr_filled, k + 1)
                act.copy(xT[:, k * 512:(k + 1) * 512].rearrange("f (q r) -> f r q", r=R),
                         tr[k % 2][:, :].rearrange("f (r q) -> f r q", r=R)).then_inc(tr_read, 1)
            for k in range(S4_BANKS):
                act.wait_ge(tr_filled, XT_BANKS + k + 1)
                act.copy(s4[:, k * 512:(k + 1) * 512], tr[(XT_BANKS + k) % 2][0:H, :]).then_inc(tr_read, 1)
            act.wait_ge(tr_filled, ST_BANK + 1)
            act.copy(sT[:, :, :], tr[ST_BANK % 2][:, 0:(N // P) * H].rearrange("p (i h) -> p i h", h=H)
                     ).then_inc(tr_read, 1)
            act.wait_ge(exp_in, 1)
            nc.scalar.activation(eA[:, :, :], trel[:, :, :], ACT.Exp).then_inc(exp_done, 1)
            nc.scalar.activation(eB[:, :, :], trel[:, :, :], ACT.Exp, scale=0.01).then_inc(exp_done, 1)
            act.wait_ge(exp_in, 2)
            nc.scalar.activation(ab[:, :, :, :], ab[:, :, :, :], ACT.Exp).then_inc(exp_done, 1)

            def evacuate(s):
                for j in range(NB_ACC):
                    if j == 0:
                        act.wait_ge(group_summed, (s + 1) * B)
                        if s >= 2:
                            act.wait_ge(combined, s - 1)
                        if s == 0:
                            act.wait_ge(a_split, H)
                            act.wait_ge(b_split, H)
                    act.copy(sums[:, s % 2, PER * j:PER * (j + 1), :].rearrange("p j (z c) -> p j z c", z=2),
                             acc[bank_of(s, j)][:, :, :, :]).then_inc(bank_read, 1)

            act.wait_ge(t_ready, 1)
            for g in range(ALLG):
                c, h, b = g // GROUPS, g // B % H, g % B
                s = g // B
                if b == 0:
                    act.wait_ge(srow_in[s % 2], 16 * (s // 2 + 1))
                if g >= CSLOTS:
                    act.wait_ge(i_ready, g - CSLOTS + 1)
                for r in range(R - dve_tiles(g)):
                    k = b * R + r
                    nc.scalar.activation(above[:, g % CSLOTS, r:CH * R:R], srow[:, s % 2, :], ACT.Sigmoid,
                                         bias=tbig[:, k, h:h + 1], scale=BIG).then_inc(act_above, 1)
                if b == EVAC_AT and s:
                    evacuate(s - 1)
            evacuate(NCH * H - 1)

        @block.vector
        def _(dve):
            made = [0]

            def link(ins):
                made[0] += 1
                ins.then_inc(dve_chain, 1)
                dve.wait_ge(dve_chain, made[0])

            def convert(k):
                dve.wait_ge(adj_in[k % 2], 16 * (k // 2 + 1))
                if k >= 2:
                    dve.wait_ge(words_turned, k - 1)
                nc.vector.tensor_scalar(edge_rows[:, k % 2, :], adj_rows[:, k % 2, :], 0.0, 0.875,
                                        ALU.is_gt, ALU.subtract, saturate=False).then_inc(rows_converted, 1)

            def store_edges(k):
                dve.wait_ge(words_turned, k + 1)
                c, n, half = k // STEPS, k // 2 % NT, k % 2
                if k % STEPS == 0 and c >= 2:
                    dve.wait_ge(group_summed, (c - 1) * GROUPS)
                to = edges[:, c % 2, half * HB:(half + 1) * HB, n * P * R:(n + 1) * P * R].bitcast(u32)
                nc.vector.tensor_scalar(to, tr[k % 2][:, :].bitcast(u32).rearrange("p (b n) -> p b n", b=HB),
                                        word(NOEDGE), word(EDGE_BITS), ALU.bitwise_xor,
                                        ALU.bitwise_and).then_inc(edges_ready, 1)

            dve.wait_ge(w_in, 16)
            dve.wait_ge(a_in, 16)
            w3 = wraw[:, :].rearrange("p (h d) -> p h d", h=H)
            link(nc.vector.tensor_tensor(wprod, w3.unsqueeze(2).broadcast_to([P, H, 2, D]), avec[:, :, :, :],
                                         ALU.mult))
            link(nc.vector.tensor_reduce(wa[:, :, :].rearrange("p k h -> p h k"), wprod, AX.X, ALU.add))
            nc.vector.tensor_copy(wx[:, :, 0:D], w3)
            nc.vector.tensor_copy(wx[:, :, D:K], wa[:, 1, :].unsqueeze(2)).then_inc(wx_ready, 1)
            convert(0)
            convert(1)

            for p in range(T // 2):
                dve.wait_ge(proj_done, p + 1)
                last = nc.vector.tensor_copy(h1[:, 2 * p:2 * p + 2, :, :],
                                             proj_bank(p).rearrange("p (t h k) -> p t h k", t=2, h=H))
                last.then_inc(proj_read, 1)
            dve.wait_ge(proj_read, T // 2)
            link(nc.vector.tensor_copy(t[:, :, :], h1[:, :, :, D]))
            nc.vector.tensor_reduce(tmax[:, :], t[:, :, :].rearrange("p t h -> p h t"), AX.X,
                                    ALU.max).then_inc(tmax_ready, 1)
            nc.vector.tensor_scalar(tneg[:, :, :], t[:, :, :], -1.0, None, ALU.mult)
            nc.vector.tensor_scalar(tbig[:, :, :], t[:, :, :], BIG, None, ALU.mult).then_inc(t_ready, 1)
            link(nc.vector.memset(h1[:, :, :, D], 1.0))
            link(nc.vector.tensor_reduce(meanw[:, :, :], h1.rearrange("p t h k -> p h k t"), AX.X, ALU.add))
            nc.vector.tensor_scalar(meanw[:, :, :], meanw[:, :, :], TINY, None, ALU.mult).then_inc(mean_ready, 1)
            dve.wait_ge(tr_filled, ST_BANK + 2)
            link(nc.vector.tensor_reduce(tcol[:, :], tr[(ST_BANK + 1) % 2][0:H, 0:P], AX.X, ALU.max))
            nc.vector.tensor_scalar(tdiag[:, :], ident[0:H, 0:H], tcol[:, :], None,
                                    ALU.mult).then_inc(tdiag_ready, 1)
            dve.wait_ge(tr_filled, ST_BANK + 3)
            link(nc.vector.tensor_copy(tall[:, :], tr[ST_BANK % 2][:, 0:H]))
            nc.vector.tensor_tensor(trel[:, :, :], t[:, :, :], tall[:, :].unsqueeze(1).broadcast_to([P, T, H]),
                                    ALU.subtract).then_inc(exp_in, 1)
            dve.wait_ge(tr_read, ST_BANK + 1)
            link(nc.vector.tensor_tensor(sT[:, :, :], sT[:, :, :],
                                         tall[:, :].unsqueeze(1).broadcast_to([P, N // P, H]), ALU.add))
            nc.vector.tensor_scalar(ab[:, :, :, 0], sT[:, :, :], 0.99, 0.0, ALU.mult, ALU.min)
            nc.vector.tensor_scalar(ab[:, :, :, 1], sT[:, :, :], -0.99, 0.0, ALU.mult,
                                    ALU.min).then_inc(exp_in, 1)

            fa = split_a.rearrange("p (t k) -> p t k", k=K)
            dve.wait_ge(exp_done, 1)
            dve.wait_ge(mean_ready, 1)
            for h in range(H):
                w = weights[:, :, h, 0:KP].rearrange("p t (c k) -> p t c k", k=K)
                if h:
                    dve.wait_ge(a_split, h)
                nc.vector.tensor_tensor(fa[:, 0:T, :], h1[:, :, h, :],
                                        eA[:, :, h:h + 1].broadcast_to([P, T, K]), ALU.mult)
                link(nc.vector.tensor_copy(fa[:, T, :], meanw[:, h, :]))
                link(nc.vector.tensor_copy(w[:, :, 0, :], fa))
                link(nc.vector.tensor_tensor(fa, fa, w[:, :, 0, :], ALU.subtract))
                link(nc.vector.tensor_copy(w[:, :, 1, :], fa))
                link(nc.vector.tensor_tensor(fa, fa, w[:, :, 1, :], ALU.subtract))
                nc.vector.tensor_copy(w[:, :, 2, :], fa).then_inc(a_split, 1)

            for k in range(STEPS):
                if k >= 2:
                    convert(k)
                store_edges(k)

            def compare(g):
                h, b, s = g // B % H, g % B, g // B
                n = dve_tiles(g)
                if n and b == 0:
                    dve.wait_ge(srow_in[s % 2], 16 * (s // 2 + 1))
                if n and g >= CSLOTS:
                    dve.wait_ge(i_ready, g - CSLOTS + 1)
                for r in range(R - n, R):
                    k = b * R + r
                    nc.vector.tensor_scalar(above[:, g % CSLOTS, r:CH * R:R], srow[:, s % 2, :],
                                            tneg[:, k, h:h + 1], None, ALU.is_ge).then_inc(dve_above, 1)

            def make_i(g):
                c, b = g // GROUPS, g % B
                dve.wait_ge(act_above, act_before[g + 1])
                dve.wait_ge(dve_above, dve_before[g + 1])
                if g % GROUPS == 0:
                    dve.wait_ge(edges_ready, STEPS * (c + 1))
                if g >= ISLOTS:
                    dve.wait_ge(group_summed, g - ISLOTS + 1)
                nc.vector.scalar_tensor_tensor(imat[:, g % ISLOTS, :].bitcast(u32),
                                               above[:, g % CSLOTS, :].bitcast(u32), I_SHIFT,
                                               edges[:, c % 2, b, :].bitcast(u32), ALU.logical_shift_left,
                                               ALU.bitwise_and).then_inc(i_ready, 1)

            def make_j(g):
                c, b = g // GROUPS, g % B
                n = j_before[g]
                dve.wait_ge(i_ready, g + 1)
                if n >= JSLOTS:
                    before = [g0 for g0 in range(g) if not j_by_matmul(g0)][n - JSLOTS]
                    dve.wait_ge(group_summed, before + 1)
                if g == 0:
                    dve.wait_ge(b_split, H)
                nc.vector.tensor_tensor(jmat[:, n % JSLOTS, :].bitcast(u32), imat[:, g % ISLOTS, :].bitcast(u32),
                                        edges[:, c % 2, b, :].bitcast(u32), ALU.bitwise_xor).then_inc(j_ready, 1)

            def row_parts(c, what):
                if what == 0:
                    dve.wait_ge(combined, H * (c + 1))
                    nc.vector.reciprocal(rden[:, :, :], heads[:, :, :, D]).then_inc(rden_ready, 1)
                elif what == 1:
                    dve.wait_ge(y_ready, c + 1)
                    link(nc.vector.tensor_reduce(mean[:, :], y[:, :, :], AX.X, ALU.add))
                    nc.vector.tensor_scalar(mean[:, :], mean[:, :], 1.0 / F, None, ALU.mult).then_inc(mean_done, 1)
                else:
                    dve.wait_ge(sq_ready, c + 1)
                    nc.vector.tensor_reduce(var[:, :], xres[:, :, :], AX.X, ALU.add).then_inc(var_done, 1)

            compare(0)
            for g in range(ALLG):
                c, gc = g // GROUPS, g % GROUPS
                if g + 1 < ALLG:
                    compare(g + 1)
                make_i(g)
                for i in range(STEPS if c + 1 < NCH else 0):
                    if STORE_AT[i] == gc:
                        store_edges((c + 1) * STEPS + i)
                    if CONVERT_AT[i] == gc:
                        convert((c + 1) * STEPS + i)
                if not j_by_matmul(g):
                    make_j(g)
                if c and gc in ROW_AT:
                    row_parts(c - 1, ROW_AT.index(gc))
            for what in range(3):
                row_parts(NCH - 1, what)

        @block.tensor
        def _(pe):
            pe.wait_ge(consts, 1)
            pe.wait_ge(x_in, 16)
            for k in range(XT_BANKS):
                if k >= 2:
                    pe.wait_ge(tr_read, k - 1)
                for r in range(R):
                    last = nc.tensor.transpose(tr[k % 2][:, r * P:(r + 1) * P], xq[:, k, r, :], ident[:, :])
                last.then_inc(tr_filled, 1)
            pe.wait_ge(wx_ready, 1)
            for k in range(S4_BANKS):
                pe.wait_ge(tr_read, XT_BANKS + max(k - 1, 0))
                nc.tensor.matmul(tr[(XT_BANKS + k) % 2][0:H, :], wa[:, 0, :], xT[:, k * 512:(k + 1) * 512],
                                 start=True, stop=True).then_inc(tr_filled, 1)
            pe.wait_ge(tr_read, ST_BANK - 1)
            for i in range(N // P):
                last = nc.tensor.matmul(tr[ST_BANK % 2][:, i * H:(i + 1) * H], xT[:, i * P:(i + 1) * P], wa[:, 0, :],
                                        start=True, stop=True)
            last.then_inc(tr_filled, 1)
            for p in range(T // 2):
                if p >= ACC:
                    pe.wait_ge(proj_read, p - ACC + 1)
                for z in range(2):
                    k = 2 * p + z
                    nodes = xT[:, (k // R) * 512 + k % R:(k // R + 1) * 512:R]
                    last = nc.tensor.matmul(proj_bank(p)[:, z * H * K:(z + 1) * H * K], nodes,
                                            wx[:, :, :].rearrange("p h k -> p (h k)"), start=True, stop=True)
                last.then_inc(proj_done, 1)
            pe.wait_ge(tmax_ready, 1)
            pe.wait_ge(tr_read, ST_BANK)
            nc.tensor.transpose(tr[(ST_BANK + 1) % 2][0:H, 0:P], tmax[:, :], ident[:, :]).then_inc(tr_filled, 1)
            pe.wait_ge(tdiag_ready, 1)
            pe.wait_ge(tr_read, ST_BANK + 1)
            nc.tensor.matmul(tr[ST_BANK % 2][:, 0:H], onesf[:, :], tdiag[:, :], start=True,
                             stop=True).then_inc(tr_filled, 1)

            def turn_words(k):
                pe.wait_ge(rows_converted, k + 1)
                if k >= 2:
                    pe.wait_ge(edges_ready, k - 1)
                for b in range(HB):
                    last = nc.tensor.transpose(tr[k % 2][:, b * P:(b + 1) * P],
                                               edge_rows[:, k % 2, b * P * R:(b + 1) * P * R].bitcast(fp32),
                                               ident[:, :])
                last.then_inc(words_turned, 1)

            pe.wait_ge(exp_in, 1)
            for k in range(STEPS):
                turn_words(k)

            for g in range(ALLG):
                c, h, b, s = g // GROUPS, g // B % H, g % B, g // B
                for i in range(STEPS if c + 1 < NCH else 0):
                    if TURN_AT[i] == g % GROUPS:
                        turn_words((c + 1) * STEPS + i)
                if b == 0 and c == 0:
                    pe.wait_ge(a_split, h + 1)
                    pe.wait_ge(b_split, h + 1)
                pe.wait_ge(i_ready, g + 1)
                if not j_by_matmul(g):
                    pe.wait_ge(j_ready, j_before[g + 1])
                for j in range(NT):
                    if b == 0 and j % PER == 0:
                        had = evacuations_before(s, j // PER)
                        if had:
                            pe.wait_ge(bank_read, had)
                        nc.tensor.matmul(acc[bank_of(s, j // PER)][:, :, :, :].rearrange("p j z c -> p j (z c)"),
                                         ones[:, :], weights[:, T, h, :].unsqueeze(1).broadcast_to([P, PER, 2 * KP]),
                                         start=True, stop=False, skip_group_check=True)
                    to = acc[bank_of(s, j // PER)][:, j % PER, :, :]
                    for r in range(R):
                        k = b * R + r
                        cols = slice(j * P * R + r, (j + 1) * P * R, R)
                        i_m = imat[:, g % ISLOTS, cols].bitcast(fp8)
                        if j_by_matmul(g):
                            nc.tensor.matmul(to.rearrange("p z c -> p (z c)"), i_m, weights[:, k, h, :],
                                             start=False, stop=False, skip_group_check=True)
                            j_m = edges[:, c % 2, b, cols].bitcast(fp8)
                        else:
                            nc.tensor.matmul(to[:, 0, :], i_m, weights[:, k, h, 0:KP],
                                             start=False, stop=False, skip_group_check=True)
                            j_m = jmat[:, j_before[g] % JSLOTS, cols].bitcast(fp8)
                        last = nc.tensor.matmul(to[:, 1, :], j_m, weights[:, k, h, KP:2 * KP], start=False,
                                                stop=(b == B - 1 and r == R - 1), skip_group_check=True)
                last.then_inc(group_summed, 1)


def kernel(x, adj, L0_gnn_W, L0_gnn_a):
    import numpy as np
    import concourse.bacc as bacc
    from concourse.bass_utils import run_bass_kernel_spmd

    nc = bacc.Bacc("TRN2", target_bir_lowering=False, num_devices=1)
    arrays = {"x": x, "adj": adj, "W": L0_gnn_W, "a": L0_gnn_a}
    arrays = {name: np.ascontiguousarray(value) for name, value in arrays.items()}
    args = [nc.dram_tensor(name, v.shape, mybir.dt.from_np(v.dtype), kind="ExternalInput").ap()
            for name, v in arrays.items()]
    heads = arrays["a"].shape[0]
    rows, features = arrays["x"].shape
    score_rows = nc.dram_tensor("score_rows", (heads, rows), mybir.dt.float32, kind="Internal").ap()
    out = nc.dram_tensor("out", (rows, features), mybir.dt.float32, kind="ExternalOutput").ap()
    graph_attention_residual_norm(nc, *args, score_rows, out)
    r = run_bass_kernel_spmd(nc, [arrays], core_ids=[0])
    return r.results[0]["out"]
```

```python
import concourse.bass as bass
from concourse import mybir
from contextlib import ExitStack


def graph_attention_residual_norm(
    nc: bass.Bass,
    x: bass.AP,
    adj: bass.AP,
    W: bass.AP,
    a: bass.AP,
    score_rows: bass.AP,
    out: bass.AP,
):
    fp32 = mybir.dt.float32
    bf16 = mybir.dt.bfloat16
    fp8 = mybir.dt.float8e4
    i32 = mybir.dt.int32
    u32 = mybir.dt.uint32
    u8 = mybir.dt.uint8
    ALU = mybir.AluOpType
    ACT = mybir.ActivationFunctionType
    AX = mybir.AxisListType

    N, F = x.shape
    H = a.shape[0]
    D = F // H
    K = D + 1
    PARTS = 3
    KP = PARTS * K
    P = 128
    R = 2
    B = N // (P * R)
    T = B * R
    GT = 4
    GB = GT // R
    G = T // GT
    CH = 1024
    NCH = N // CH
    NT = CH // P
    HB = B // 2
    HALF = N // 2
    STEPS = 2 * NT
    GROUPS = H * G
    ALLG = NCH * GROUPS
    ACC = 6
    PER = 2
    BANK = 512
    NB_ACC = NT // PER
    READS = NB_ACC // 2
    DVE_TILES = (1,)
    BY_MATMUL = (0, 1)
    ACT_STORES = tuple(range(0, STEPS, 2))
    CONVERT_SPAN = GROUPS - 8
    DVE_STORE_LAG, ACT_STORE_LAG = 4, 6
    JOIN_AT = 2
    FINISH_AT = (4, 6)
    X_AT = 10
    S4_AFTER = 8
    CONVERT_FIRST = 5
    BIG = float(2 ** 60)
    TINY = float(2.0 ** -100)
    EPS = 1e-5
    CSLOTS, ISLOTS, JSLOTS = 4, 3, 3
    EDGE, I_SHIFT = -0.125, 5
    XSUMS = N // BANK

    CONVERT_AT = [i * CONVERT_SPAN // (STEPS - 1) for i in range(STEPS)]
    TURN_AT = [at + 1 for at in CONVERT_AT]
    STORE_AT = [at + (ACT_STORE_LAG if i in ACT_STORES else DVE_STORE_LAG) for i, at in enumerate(CONVERT_AT)]
    LATE_STORES = {0: (12, 13), 1: (14,), 2: (15,)}

    def dve_tiles(g):
        return DVE_TILES[g % len(DVE_TILES)]

    def j_by_matmul(g):
        return bool(BY_MATMUL[g % len(BY_MATMUL)])

    def act_stores(k):
        return k < STEPS or k % STEPS in ACT_STORES

    def stores_before(k, by_act):
        return sum(act_stores(i) == by_act for i in range(k))

    act_before = [0]
    dve_before = [0]
    j_groups = [g for g in range(ALLG) if not j_by_matmul(g)]
    j_before = [0]
    for g in range(ALLG):
        act_before.append(act_before[-1] + GT - dve_tiles(g))
        dve_before.append(dve_before[-1] + dve_tiles(g))
        j_before.append(j_before[-1] + (not j_by_matmul(g)))

    def bank_of(s, j):
        return ((s % H) * NB_ACC + j) % ACC

    def reads_before(s, j):
        had = [(s0, j0) for s0 in range(s) for j0 in range(NB_ACC) if bank_of(s0, j0) == bank_of(s, j)]
        return had[-1][0] * READS + had[-1][1] // 2 + 1 if had else None

    ctx = ExitStack()
    with ctx:
        def sb(name, shape, dt):
            return ctx.enter_context(nc.sbuf_tensor(name, shape, dt))

        def pb(name, shape, dt):
            return ctx.enter_context(nc.psum_tensor(name, shape, dt))

        def sem(name):
            return ctx.enter_context(nc.semaphore(name))

        adj_rows = sb("adj_rows", [P, 2, HALF], i32)
        edge_rows = sb("edge_rows", [P, 2, HALF], fp8)
        edges = sb("edges", [P, 2, G, GB * CH * R], u8)
        above = sb("above", [P, CSLOTS, GB * CH * R], u8)
        ij = sb("ij", [P, ISLOTS + JSLOTS, GB * CH * R], u8)
        imat, jmat = ij[:, 0:ISLOTS, :], ij[:, ISLOTS:, :]
        weights = sb("weights", [P, T + 1, H, 2 * KP], bf16)
        srow = sb("srow", [P, 2, CH], fp32)
        heads = sb("heads", [P, NT, H, K], fp32)
        joined = sb("joined", [P, NT, 2, K], fp32)
        y = sb("y", [P, NT, F], fp32)
        rden = sb("rden", [P, NT, H], fp32)
        stats = sb("stats", [P, NT, 6], fp32)
        moments = sb("moments", [P, NT, 2], fp32)
        rstd = sb("rstd", [P, NT], fp32)
        power = sb("power", [P, NT], fp32)
        ident = sb("ident", [P, P], fp32)
        ident16 = sb("ident16", [P, P], bf16)
        ones = sb("ones", [P, P], bf16)
        onesf = sb("onesf", [H, P], fp32)
        wraw = sb("wraw", [P, F], fp32)
        avec = sb("avec", [P, H, 2, D], fp32)
        wprod = sb("wprod", [P, H, 2, D], fp32)
        wa = sb("wa", [P, 2, H], fp32)
        wx = sb("wx", [P, H * K + H], fp32)
        xsum = sb("xsum", [P, XSUMS], fp32)
        t = sb("t", [P, T, H], fp32)
        tneg = sb("tneg", [P, T, H], fp32)
        tbig = sb("tbig", [P, T, H], fp32)
        eA = sb("eA", [P, T, H], fp32)
        eB = sb("eB", [P, T, H], fp32)
        ab = sb("ab", [P, T, H, 2], fp32)
        tmax = sb("tmax", [P, H], fp32)
        tcol = sb("tcol", [H, 1], fp32)
        tdiag = sb("tdiag", [H, H], fp32)
        tall = sb("tall", [P, H], fp32)
        meanw = sb("meanw", [P, H, K], fp32)
        split = sb("split", [P, T * K], fp32)

        ij32 = ij[:, :, :].rearrange("p s c -> p (s c)").bitcast(fp32)
        WIDE = H * K + H
        features = ij32[:, 0:T * WIDE].rearrange("p (t c) -> p t c", t=T)
        h1 = features[:, :, 0:H * K].rearrange("p t (h k) -> p t h k", h=H)
        s_rows = features[:, :, H * K:]
        late_above = above[:, CSLOTS - 3:, :].rearrange("p s c -> p (s c)").bitcast(fp32)[:, 0:2 * T * K].rearrange(
            "p (z c) -> p z c", z=2)

        def split_a(h):
            return late_above[:, h % 2, :].rearrange("p (t k) -> p t k", k=K)

        def split_b(h):
            at = (split[:, :], ij32[:, T * WIDE:T * WIDE + T * K])[h % 2]
            return at.rearrange("p (t k) -> p t k", k=K)

        def part_of(h, side, part):
            return weights[:, 0:T, h, side * KP + part * K:side * KP + (part + 1) * K]
        early = edges[:, 1, :, :].rearrange("p g c -> p (g c)").bitcast(fp32)
        xq = early[:, 0:T * F].rearrange("p (b r f) -> p b r f", b=B, r=R)
        xT = early[:, T * F:2 * T * F]
        s4 = early[0:H, 0:N]

        acc_all = pb("acc_all", [P, ACC, PER, BANK // PER], fp32)
        acc = acc_all[:, :, :, 0:2 * KP]
        tr = [pb(f"tr{i}", [P, 2 * BANK], bf16) for i in range(2)]

        def columns(i, j):
            first = (i // R) * CH * R + i % R
            if j is None:
                return slice(first, first + CH * R - R + 1, R)
            return slice(first + j * P * R, first + (j + 1) * P * R - R + 1, R)

        def start_bank(u):
            return acc_all[:, u % ACC, :, :].rearrange("p j c -> p (j c)")

        U_XT = 0
        U_PROJ = U_XT + N // BANK
        U_MEAN = U_PROJ + T // 2
        U_TMAX = U_MEAN + 1
        U_TALL = U_TMAX + 1
        U_S4 = U_TALL + 1
        U_ALL = U_S4 + N // BANK
        VECTOR_READS = (U_MEAN, U_TMAX, U_TALL)

        x_in, w_in, a_in, y_in = sem("x_in"), sem("w_in"), sem("a_in"), sem("y_in")
        adj_in = [sem(f"adj_in{i}") for i in range(2)]
        srow_in = [sem(f"srow_in{i}") for i in range(2)]
        s4_out, y_out = sem("s4_out"), sem("y_out")
        ident_ready, consts_ready = sem("ident_ready"), sem("consts_ready")
        pool_chain = sem("pool_chain")
        dve_chain = sem("dve_chain")
        wx_ready = sem("wx_ready")
        start_filled = sem("start_filled")
        start_read_act = sem("start_read_act")
        start_read_dve = sem("start_read_dve")
        tmax_ready, tdiag_ready = sem("tmax_ready"), sem("tdiag_ready")
        t_ready = sem("t_ready")
        exp_in, exp_done = sem("exp_in"), sem("exp_done")
        a_residual1, a_residual2 = sem("a_residual1"), sem("a_residual2")
        b_product = sem("b_product")
        b_residual1, b_residual2 = sem("b_residual1"), sem("b_residual2")
        b_high = sem("b_high")
        a_middle, b_middle = sem("a_middle"), sem("b_middle")
        a_split, b_split = sem("a_split"), sem("b_split")
        mean_split = sem("mean_split")
        rows_converted = sem("rows_converted")
        words_turned = sem("words_turned")
        stored_act, stored_dve = sem("stored_act"), sem("stored_dve")
        act_above, dve_above = sem("act_above"), sem("dve_above")
        i_ready, j_ready = sem("i_ready"), sem("j_ready")
        group_summed = sem("group_summed")
        sums_read = sem("sums_read")
        rden_ready, added = sem("rden_ready"), sem("added")
        moments_ready, rstd_ready, y_normed = sem("moments_ready"), sem("rstd_ready"), sem("y_normed")

        def store_place(k):
            c, n, half = k // STEPS, k // 2 % NT, k % 2
            blocks = edges[:, c % 2, :, :].rearrange("p g (b x) -> p (g b) x", b=GB)
            return blocks[:, half * HB:(half + 1) * HB, n * P * R:(n + 1) * P * R]

        def start_was_read(eng, u):
            if u in VECTOR_READS:
                eng.wait_ge(start_read_dve, sum(v <= u for v in VECTOR_READS))
            else:
                eng.wait_ge(start_read_act, u + 1 - sum(v < u for v in VECTOR_READS))

        def was_stored(eng, k):
            eng.wait_ge(stored_act if act_stores(k) else stored_dve, stores_before(k + 1, act_stores(k)))

        block = ctx.enter_context(nc.Block())

        x_tiles = x.rearrange("(b q r) f -> q b (r f)", q=P, r=R)
        x_rows = x.rearrange("(c b q r) f -> c q b r f", c=NCH, q=P, r=R)
        out_rows = out.rearrange("(c b q r) f -> c q b r f", c=NCH, q=P, r=R)
        y_rows = y[:, :, :].rearrange("p (b r) f -> p b r f", r=R)
        adj_tiles = adj.rearrange("(b q r) m -> b r q m", q=P, r=R)

        @block.sync
        def _(sp):
            sp.dma_start(xq.rearrange("p b r f -> p b (r f)"), x_tiles).then_inc(x_in, 16)
            sp.dma_start(wraw[:, :], W).then_inc(w_in, 16)
            sp.dma_start(avec[:, :, :, :].rearrange("p h k d -> p (h k d)"),
                         a.rearrange("h e o -> (h e o)").partition_broadcast(P)).then_inc(a_in, 16)

            def load_adj(k):
                if k >= 2:
                    sp.wait_ge(rows_converted, k - 1)
                n, half = k // 2, k % 2
                sp.dma_start(adj_rows[:, k % 2, :],
                             adj_tiles[n // R, n % R, :, half * HALF:(half + 1) * HALF]).then_inc(adj_in[k % 2], 16)

            def load_srow(s):
                c, h = s // H, s % H
                if s >= 2:
                    sp.wait_ge(act_above, act_before[(s - 1) * G])
                    sp.wait_ge(dve_above, dve_before[(s - 1) * G])
                sp.dma_start(srow[:, s % 2, :],
                             score_rows[h, c * CH:(c + 1) * CH].partition_broadcast(P)).then_inc(srow_in[s % 2], 16)

            for k in range(S4_AFTER):
                load_adj(k)
            start_was_read(sp, U_ALL - 1)
            sp.dma_start(score_rows, s4).then_inc(s4_out, 16)
            load_adj(S4_AFTER)
            sp.wait_ge(s4_out, 16)
            load_srow(0)
            load_srow(1)
            sp.dma_start(y_rows, x_rows[0]).then_inc(y_in, 16)
            for k in range(S4_AFTER + 1, STEPS + 2):
                load_adj(k)
            for g in range(ALLG):
                c, gc, s = g // GROUPS, g % GROUPS, g // G
                if g % G == 0 and s >= 1 and s + 1 < NCH * H:
                    load_srow(s + 1)
                for i in range(STEPS):
                    k = (c + 1) * STEPS + i + 2
                    if CONVERT_AT[i] == gc and k < NCH * STEPS:
                        load_adj(k)
                if gc == X_AT and c:
                    sp.wait_ge(y_normed, c)
                    sp.dma_start(out_rows[c - 1], y_rows).then_inc(y_out, 16)
                    sp.wait_ge(y_out, 16 * c)
                    sp.dma_start(y_rows, x_rows[c]).then_inc(y_in, 16)
            sp.wait_ge(y_normed, NCH)
            sp.dma_start(out_rows[NCH - 1], y_rows).then_inc(y_out, 16)
            sp.wait_ge(y_out, 16 * NCH)

        @block.gpsimd
        def _(pool):
            made = [0]

            def link(ins):
                made[0] += 1
                ins.then_inc(pool_chain, 1)
                pool.wait_ge(pool_chain, made[0])

            link(pool.memset(ident[:, :], 0.0))
            pool.affine_select(out=ident[:, :], in_=ident[:, :], compare_op=ALU.not_equal, fill=1.0,
                               base=0, pattern=[[-1, P]], channel_multiplier=1).then_inc(ident_ready, 1)
            pool.wait_ge(ident_ready, 1)
            link(pool.tensor_copy(ident16[:, :], ident[:, :]))
            link(pool.memset(ones[:, :], 1.0))
            link(pool.memset(power[:, :], -0.5))
            link(pool.memset(meanw[:, :, :], 0.0))
            pool.memset(onesf[:, :], 1.0).then_inc(consts_ready, 1)

            pool.wait_ge(exp_done, 2)
            link(pool.tensor_scalar(eB[:, :, :], eB[:, :, :], -1.0, 0.0, ALU.mult, ALU.add))
            for pair in range(0, H, 2):
                for h in (pair, pair + 1):
                    if h >= 2:
                        pool.wait_ge(b_split, h - 1)
                    pool.tensor_tensor(split_b(h), h1[:, :, h, :],
                                       eB[:, :, h:h + 1].broadcast_to([P, T, K]), ALU.mult).then_inc(b_product, 1)
                for part in range(2):
                    for h in (pair, pair + 1):
                        pool.wait_ge((b_high, b_middle)[part], h + 1)
                        pool.tensor_tensor(split_b(h), split_b(h), part_of(h, 1, part),
                                           ALU.subtract).then_inc((b_residual1, b_residual2)[part], 1)

            for c in range(NCH):
                pool.wait_ge(moments_ready, c + 1)
                link(pool.tensor_scalar(rstd[:, :], moments[:, :, 1], 1.0, EPS, ALU.mult, ALU.add))
                pool.tensor_tensor(rstd[:, :], rstd[:, :], power[:, :], ALU.pow).then_inc(rstd_ready, 1)

        @block.scalar
        def _(act):
            def store_edges(k):
                act.wait_ge(words_turned, k + 1)
                c = k // STEPS
                if k == STEPS + min(ACT_STORES, default=0):
                    act.wait_ge(start_filled, U_ALL)
                    act.wait_ge(s4_out, 16)
                if c >= 2:
                    act.wait_ge(group_summed, (c - 1) * GROUPS)
                act.copy(store_place(k).bitcast(fp32), tr[k % 2][:, :].bitcast(fp32).rearrange("p (b n) -> p b n", b=HB)
                         ).then_inc(stored_act, 1)

            for k in range(N // BANK):
                act.wait_ge(start_filled, U_XT + k + 1)
                nc.scalar.activation(xT[:, k * BANK:(k + 1) * BANK], start_bank(U_XT + k), ACT.Identity,
                                     accum_out=xsum[:, k:k + 1]).then_inc(start_read_act, 1)
            for p in range(T // 2):
                if p % 8 == 0:
                    store_edges(p // 4)
                    store_edges(p // 4 + 1)
                act.wait_ge(start_filled, U_PROJ + p + 1)
                act.copy(features[:, 2 * p:2 * p + 2, :].rearrange("p t c -> p (t c)"),
                         start_bank(U_PROJ + p)[:, 0:2 * WIDE]).then_inc(start_read_act, 1)
            act.wait_ge(exp_in, 1)
            nc.scalar.activation(eA[:, :, :], eA[:, :, :], ACT.Exp).then_inc(exp_done, 1)
            nc.scalar.activation(eB[:, :, :], eB[:, :, :], ACT.Exp, scale=0.01).then_inc(exp_done, 1)
            for k in range(N // BANK):
                act.wait_ge(start_filled, U_S4 + k + 1)
                act.copy(s4[:, k * BANK:(k + 1) * BANK], start_bank(U_S4 + k)[0:H, :]).then_inc(start_read_act, 1)
                if k % 4 == 3:
                    store_edges(4 + k // 2 - 1)
                    store_edges(4 + k // 2)

            early_stores = list(range(8, min(LATE_STORES[0])))
            for pair in range(0, H, 2):
                for part in range(PARTS):
                    for h in (pair, pair + 1):
                        if part:
                            act.wait_ge((a_residual1, a_residual2)[part - 1], h + 1)
                            act.copy(part_of(h, 0, part), split_a(h)).then_inc((a_middle, a_split)[part - 1], 1)
                        act.wait_ge((b_product, b_residual1, b_residual2)[part], h + 1)
                        act.copy(part_of(h, 1, part), split_b(h)).then_inc((b_high, b_middle, b_split)[part], 1)
                    if early_stores and part == 1:
                        store_edges(early_stores.pop(0))
                if pair == 0:
                    act.wait_ge(exp_in, 2)
                    nc.scalar.activation(ab[:, :, :, :], ab[:, :, :, :], ACT.Exp).then_inc(exp_done, 1)
            for k in early_stores:
                store_edges(k)

            act.wait_ge(t_ready, 1)
            for g in range(ALLG):
                c, gc, h, b, s = g // GROUPS, g % GROUPS, g // G % H, g % G, g // G
                if b == 0:
                    act.wait_ge(srow_in[s % 2], 16 * (s // 2 + 1))
                if g == 1:
                    act.wait_ge(a_split, H)
                if g >= CSLOTS:
                    act.wait_ge(i_ready, g - CSLOTS + 1)
                for i in range(GT - dve_tiles(g)):
                    nc.scalar.activation(above[:, g % CSLOTS, columns(i, None)], srow[:, s % 2, :], ACT.Sigmoid,
                                         bias=tbig[:, b * GT + i, h:h + 1], scale=BIG).then_inc(act_above, 1)
                for k in LATE_STORES.get(g, ()):
                    store_edges(k)
                for i in range(STEPS if c + 1 < NCH else 0):
                    if STORE_AT[i] == gc and act_stores(STEPS + i):
                        store_edges((c + 1) * STEPS + i)

        @block.vector
        def _(dve):
            made = [0]

            def link(ins):
                made[0] += 1
                ins.then_inc(dve_chain, 1)
                dve.wait_ge(dve_chain, made[0])

            def convert(k):
                dve.wait_ge(adj_in[k % 2], 16 * (k // 2 + 1))
                if k >= 2:
                    dve.wait_ge(words_turned, k - 1)
                nc.vector.tensor_scalar(edge_rows[:, k % 2, :], adj_rows[:, k % 2, :], 0.0, EDGE,
                                        ALU.is_gt, ALU.mult, saturate=False).then_inc(rows_converted, 1)

            def store_edges(k):
                dve.wait_ge(words_turned, k + 1)
                c = k // STEPS
                if c == 1:
                    dve.wait_ge(start_filled, U_ALL)
                    dve.wait_ge(s4_out, 16)
                if c >= 2:
                    dve.wait_ge(group_summed, (c - 1) * GROUPS)
                nc.vector.tensor_copy(store_place(k).bitcast(u32), tr[k % 2][:, :].bitcast(u32).rearrange("p (b n) -> p b n", b=HB)
                                      ).then_inc(stored_dve, 1)

            dve.wait_ge(w_in, 16)
            dve.wait_ge(a_in, 16)
            w3 = wraw[:, :].rearrange("p (h d) -> p h d", h=H)
            link(nc.vector.tensor_tensor(wprod[:, :, :, :], w3.unsqueeze(2).broadcast_to([P, H, 2, D]),
                                         avec[:, :, :, :], ALU.mult))
            link(nc.vector.tensor_reduce(wa[:, :, :].rearrange("p k h -> p h k"), wprod[:, :, :, :], AX.X, ALU.add))
            by_head = wx[:, 0:H * K].rearrange("p (h k) -> p h k", h=H)
            nc.vector.tensor_copy(by_head[:, :, 0:D], w3)
            nc.vector.tensor_copy(by_head[:, :, D], wa[:, 1, :])
            nc.vector.tensor_copy(wx[:, H * K:], wa[:, 0, :]).then_inc(wx_ready, 1)
            for k in range(CONVERT_FIRST):
                convert(k)

            start_was_read(dve, U_MEAN - 1)
            link(nc.vector.tensor_copy(t[:, :, :], h1[:, :, :, D]))
            nc.vector.tensor_reduce(tmax[:, :], t[:, :, :].rearrange("p t h -> p h t"), AX.X,
                                    ALU.max).then_inc(tmax_ready, 1)
            nc.vector.memset(h1[:, :, :, D], 1.0)
            dve.wait_ge(consts_ready, 1)
            dve.wait_ge(start_filled, U_MEAN + 1)
            link(nc.vector.tensor_scalar(meanw[0:XSUMS, :, :].rearrange("p h k -> p (h k)"),
                                         start_bank(U_MEAN)[0:XSUMS, 0:H * K], TINY, None,
                                         ALU.mult))
            link(nc.vector.memset(meanw[0:XSUMS, :, D], TINY * (N // XSUMS)))
            dve.wait_ge(start_filled, U_TMAX + 1)
            link(nc.vector.tensor_reduce(tcol[:, :], start_bank(U_TMAX)[0:H, 0:P], AX.X, ALU.max))
            nc.vector.tensor_scalar(tdiag[:, :], ident[0:H, 0:H], tcol[:, :], None,
                                    ALU.mult).then_inc(tdiag_ready, 1)
            dve.sem_inc(start_read_dve, 2)
            nc.vector.tensor_scalar(tneg[:, :, :], t[:, :, :], -1.0, None, ALU.mult)
            nc.vector.tensor_scalar(tbig[:, :, :], t[:, :, :], BIG, None, ALU.mult).then_inc(t_ready, 1)
            both = weights[:, T, :, :].rearrange("p h (z c k) -> p h z c k", z=2, k=K)
            for part in range(PARTS):
                link(nc.vector.tensor_copy(both[:, :, :, part, :], meanw[:, :, :].unsqueeze(2).broadcast_to([P, H, 2, K])))
                if part < PARTS - 1:
                    link(nc.vector.tensor_tensor(meanw[:, :, :], meanw[:, :, :], both[:, :, 0, part, :], ALU.subtract))
            nc.vector.sem_inc(mean_split, 1)
            convert(CONVERT_FIRST)
            dve.wait_ge(start_filled, U_TALL + 1)
            nc.vector.tensor_copy(tall[:, :], start_bank(U_TALL)[:, 0:H]).then_inc(start_read_dve, 1)
            dve.wait_ge(start_read_dve, len(VECTOR_READS))
            for to in (eA, eB):
                last = nc.vector.tensor_tensor(to[:, :, :], t[:, :, :],
                                               tall[:, :].unsqueeze(1).broadcast_to([P, T, H]), ALU.subtract)
            last.then_inc(exp_in, 1)

            def compare(g):
                h, b, s = g // G % H, g % G, g // G
                n = dve_tiles(g)
                if n and b < 2:
                    dve.wait_ge(srow_in[s % 2], 16 * (s // 2 + 1))
                if n and g == 1:
                    dve.wait_ge(a_split, H)
                if n and g >= CSLOTS:
                    dve.wait_ge(i_ready, g - CSLOTS + 1)
                for i in range(GT - n, GT):
                    nc.vector.tensor_scalar(above[:, g % CSLOTS, columns(i, None)], srow[:, s % 2, :],
                                            tneg[:, b * GT + i, h:h + 1], None, ALU.is_ge).then_inc(dve_above, 1)

            dve.wait_ge(exp_done, 1)
            todo = list(range(CONVERT_FIRST + 1, STEPS))
            for pair in range(0, H, 2):
                for h in (pair, pair + 1):
                    if h >= 2:
                        dve.wait_ge(a_split, h - 1)
                    link(nc.vector.tensor_tensor(split_a(h), h1[:, :, h, :],
                                                 eA[:, :, h:h + 1].broadcast_to([P, T, K]), ALU.mult))
                    link(nc.vector.tensor_copy(part_of(h, 0, 0), split_a(h)))
                    nc.vector.tensor_tensor(split_a(h), split_a(h), part_of(h, 0, 0),
                                            ALU.subtract).then_inc(a_residual1, 1)
                convert(todo.pop(0))
                convert(todo.pop(0))
                for h in (pair, pair + 1):
                    dve.wait_ge(a_middle, h + 1)
                    nc.vector.tensor_tensor(split_a(h), split_a(h), part_of(h, 0, 1),
                                            ALU.subtract).then_inc(a_residual2, 1)
                convert(todo.pop(0))
                if pair == 0:
                    convert(todo.pop(0))
                    link(nc.vector.tensor_tensor(s_rows, s_rows, tall[:, :].unsqueeze(1).broadcast_to([P, T, H]),
                                                 ALU.add))
                    nc.vector.tensor_scalar(ab[:, :, :, 0], s_rows, 0.99, 0.0, ALU.mult, ALU.min)
                    nc.vector.tensor_scalar(ab[:, :, :, 1], s_rows, -0.99, 0.0, ALU.mult,
                                            ALU.min).then_inc(exp_in, 1)
            for k in todo:
                convert(k)

            def make_i(g):
                c, b = g // GROUPS, g % G
                dve.wait_ge(act_above, act_before[g + 1])
                dve.wait_ge(dve_above, dve_before[g + 1])
                if g % GROUPS == 0:
                    dve.wait_ge(stored_act, stores_before(STEPS * (c + 1), True))
                    if c and stores_before(STEPS * (c + 1), False):
                        dve.wait_ge(stored_dve, stores_before(STEPS * (c + 1), False))
                if g == 0:
                    dve.wait_ge(a_split, H)
                    dve.wait_ge(b_split, H)
                if g >= ISLOTS:
                    dve.wait_ge(group_summed, g - ISLOTS + 1)
                nc.vector.scalar_tensor_tensor(imat[:, g % ISLOTS, :].bitcast(u32),
                                               above[:, g % CSLOTS, :].bitcast(u32), I_SHIFT,
                                               edges[:, c % 2, b, :].bitcast(u32), ALU.logical_shift_left,
                                               ALU.bitwise_and).then_inc(i_ready, 1)

            def make_j(g):
                c, b = g // GROUPS, g % G
                n = j_before[g]
                dve.wait_ge(i_ready, g + 1)
                if n >= JSLOTS:
                    dve.wait_ge(group_summed, j_groups[n - JSLOTS] + 1)
                nc.vector.tensor_tensor(jmat[:, n % JSLOTS, :].bitcast(u32), imat[:, g % ISLOTS, :].bitcast(u32),
                                        edges[:, c % 2, b, :].bitcast(u32), ALU.bitwise_xor).then_inc(j_ready, 1)

            def join(s):
                c, h = s // H, s % H
                dve.wait_ge(group_summed, (s + 1) * G)
                for i in range(READS):
                    first = bank_of(s, 2 * i)
                    view = acc[:, first:first + 2, :, :].rearrange("p b j (z c k) -> p (b j) z k c", z=2, k=K)
                    nc.vector.tensor_reduce(joined[:, i * NT // READS:(i + 1) * NT // READS, :, :], view, AX.X,
                                            ALU.add).then_inc(sums_read, 1)
                dve.wait_ge(sums_read, (s + 1) * READS)
                if s == 0:
                    dve.wait_ge(exp_done, 3)
                rows = ab[:, c * NT:(c + 1) * NT, h, :]
                link(nc.vector.tensor_tensor(joined[:, :, :, :], joined[:, :, :, :],
                                             rows.unsqueeze(3).broadcast_to([P, NT, 2, K]), ALU.mult))
                link(nc.vector.tensor_tensor(heads[:, :, h, :], joined[:, :, 0, :], joined[:, :, 1, :], ALU.add))

            def finish(c, part):
                if part == 0:
                    link(nc.vector.reciprocal(rden[:, :, :], heads[:, :, :, D]))
                    link(nc.vector.tensor_tensor(heads[:, :, :, 0:D], heads[:, :, :, 0:D],
                                                 rden[:, :, :].unsqueeze(3).broadcast_to([P, NT, H, D]), ALU.mult))
                    dve.wait_ge(y_in, 16 * (c + 1))
                    y4 = y[:, :, :].rearrange("p j (h d) -> p j h d", h=H)
                    link(nc.vector.tensor_tensor(y4, y4, heads[:, :, :, 0:D], ALU.add))
                    for j in range(NT):
                        last = nc.vector.bn_stats(stats[:, j, :], y[:, j, :])
                    link(last)
                    for j in range(NT):
                        last = nc.vector.bn_aggr(moments[:, j, :], stats[:, j, :])
                    last.then_inc(moments_ready, 1)
                else:
                    dve.wait_ge(rstd_ready, c + 1)
                    for j in range(NT):
                        last = nc.vector.tensor_scalar(y[:, j, :], y[:, j, :], moments[:, j, 0:1], rstd[:, j:j + 1],
                                                       ALU.subtract, ALU.mult)
                    last.then_inc(y_normed, 1)

            compare(0)
            for g in range(ALLG):
                c, gc, b, s = g // GROUPS, g % GROUPS, g % G, g // G
                if g + 1 < ALLG:
                    compare(g + 1)
                make_i(g)
                for i in range(STEPS if c + 1 < NCH else 0):
                    if STORE_AT[i] == gc and not act_stores(STEPS + i):
                        store_edges((c + 1) * STEPS + i)
                    if CONVERT_AT[i] == gc:
                        convert((c + 1) * STEPS + i)
                if b == JOIN_AT and s:
                    join(s - 1)
                if not j_by_matmul(g):
                    make_j(g)
                if c and gc in FINISH_AT:
                    finish(c - 1, FINISH_AT.index(gc))
            join(NCH * H - 1)
            finish(NCH - 1, 0)
            finish(NCH - 1, 1)

        @block.tensor
        def _(pe):
            def turn_words(k):
                pe.wait_ge(rows_converted, k + 1)
                if k >= 2:
                    was_stored(pe, k - 2)
                for b in range(HB):
                    last = nc.tensor.transpose(tr[k % 2][:, b * P:(b + 1) * P],
                                               edge_rows[:, k % 2, b * P * R:(b + 1) * P * R].bitcast(bf16),
                                               ident16[:, :])
                last.then_inc(words_turned, 1)

            def free_bank(u):
                if u >= ACC:
                    start_was_read(pe, u - ACC)
                return start_bank(u)

            pe.wait_ge(ident_ready, 1)
            pe.wait_ge(x_in, 16)
            for k in range(N // BANK):
                to = free_bank(U_XT + k)
                for i in range(GT):
                    last = nc.tensor.transpose(to[:, i * P:(i + 1) * P], xq[:, k * GB + i // R, i % R, :], ident[:, :])
                last.then_inc(start_filled, 1)
            pe.wait_ge(wx_ready, 1)
            pe.wait_ge(consts_ready, 1)
            for p in range(T // 2):
                if p % 8 == 0:
                    turn_words(p // 4)
                    turn_words(p // 4 + 1)
                to = free_bank(U_PROJ + p)
                start_was_read(pe, U_XT + p // 2)
                for z in range(2):
                    k = 2 * p + z
                    last = nc.tensor.matmul(to[:, z * WIDE:(z + 1) * WIDE], xT[:, k * P:(k + 1) * P], wx[:, :],
                                            start=True, stop=True)
                last.then_inc(start_filled, 1)
            nc.tensor.matmul(free_bank(U_MEAN)[0:XSUMS, 0:H * K], xsum[:, :],
                             wx[:, 0:H * K], start=True, stop=True).then_inc(start_filled, 1)
            to = free_bank(U_TMAX)
            pe.wait_ge(tmax_ready, 1)
            nc.tensor.transpose(to[0:H, 0:P], tmax[:, :], ident[:, :]).then_inc(start_filled, 1)
            to = free_bank(U_TALL)
            pe.wait_ge(tdiag_ready, 1)
            nc.tensor.matmul(to[:, 0:H], onesf[:, :], tdiag[:, :], start=True, stop=True).then_inc(start_filled, 1)
            for k in range(N // BANK):
                nc.tensor.matmul(free_bank(U_S4 + k)[0:H, :], wa[:, 0, :], xT[:, k * BANK:(k + 1) * BANK],
                                 start=True, stop=True).then_inc(start_filled, 1)
                if k % 4 == 3:
                    turn_words(4 + k // 2 - 1)
                    turn_words(4 + k // 2)
            for k in range(8, STEPS):
                turn_words(k)
            for u in range(U_ALL - ACC, U_ALL):
                start_was_read(pe, u)

            for g in range(ALLG):
                c, gc, h, b, s = g // GROUPS, g % GROUPS, g // G % H, g % G, g // G
                for i in range(STEPS if c + 1 < NCH else 0):
                    if TURN_AT[i] == gc:
                        turn_words((c + 1) * STEPS + i)
                if b == 0 and c == 0:
                    if h == 0:
                        pe.wait_ge(mean_split, 1)
                    pe.wait_ge(a_split, h + 1)
                    pe.wait_ge(b_split, h + 1)
                pe.wait_ge(i_ready, g + 1)
                if not j_by_matmul(g):
                    pe.wait_ge(j_ready, j_before[g + 1])
                for j in range(NT):
                    bank = bank_of(s, j // PER)
                    if b == 0 and j % PER == 0:
                        had = reads_before(s, j // PER)
                        if had:
                            pe.wait_ge(sums_read, had)
                        nc.tensor.matmul(acc[:, bank, :, :], ones[:, :],
                                         weights[:, T, h, :].unsqueeze(1).broadcast_to([P, PER, 2 * KP]),
                                         start=True, stop=False, skip_group_check=True)
                    to = acc[:, bank, j % PER, :]
                    for i in range(GT):
                        k = b * GT + i
                        cols = columns(i, j)
                        i_m = imat[:, g % ISLOTS, cols].bitcast(fp8)
                        if j_by_matmul(g):
                            nc.tensor.matmul(to, i_m, weights[:, k, h, :], start=False, stop=False,
                                             skip_group_check=True)
                            j_m = edges[:, c % 2, b, cols].bitcast(fp8)
                        else:
                            nc.tensor.matmul(to[:, 0:KP], i_m, weights[:, k, h, 0:KP], start=False, stop=False,
                                             skip_group_check=True)
                            j_m = jmat[:, j_before[g] % JSLOTS, cols].bitcast(fp8)
                        last = nc.tensor.matmul(to[:, KP:2 * KP], j_m, weights[:, k, h, KP:2 * KP], start=False,
                                                stop=(b == G - 1 and i == GT - 1), skip_group_check=True)
                last.then_inc(group_summed, 1)


def kernel(x, adj, L0_gnn_W, L0_gnn_a):
    import numpy as np
    import concourse.bacc as bacc
    from concourse.bass_utils import run_bass_kernel_spmd

    nc = bacc.Bacc("TRN2", target_bir_lowering=False, num_devices=1)
    arrays = {"x": x, "adj": adj, "W": L0_gnn_W, "a": L0_gnn_a}
    arrays = {name: np.ascontiguousarray(value) for name, value in arrays.items()}
    args = [nc.dram_tensor(name, v.shape, mybir.dt.from_np(v.dtype), kind="ExternalInput").ap()
            for name, v in arrays.items()]
    heads = arrays["a"].shape[0]
    rows, features = arrays["x"].shape
    score_rows = nc.dram_tensor("score_rows", (heads, rows), mybir.dt.float32, kind="Internal").ap()
    out = nc.dram_tensor("out", (rows, features), mybir.dt.float32, kind="ExternalOutput").ap()
    graph_attention_residual_norm(nc, *args, score_rows, out)
    r = run_bass_kernel_spmd(nc, [arrays], core_ids=[0])
    return r.results[0]["out"]
```

```python
import concourse.bass as bass
from concourse import mybir
from contextlib import ExitStack


def graph_attention_residual_norm(
    nc: bass.Bass,
    x: bass.AP,
    adj: bass.AP,
    W: bass.AP,
    a: bass.AP,
    score_rows: bass.AP,
    out: bass.AP,
):
    fp32 = mybir.dt.float32
    bf16 = mybir.dt.bfloat16
    fp8 = mybir.dt.float8e4
    i32 = mybir.dt.int32
    u32 = mybir.dt.uint32
    u8 = mybir.dt.uint8
    ALU = mybir.AluOpType
    ACT = mybir.ActivationFunctionType
    AX = mybir.AxisListType

    N, F = x.shape
    H = a.shape[0]
    D = F // H
    K = D + 1
    PARTS = 3
    KP = PARTS * K
    P = 128
    R = 2
    B = N // (P * R)
    T = B * R
    GT = 4
    GB = GT // R
    G = T // GT
    CH = 1024
    NCH = N // CH
    NT = CH // P
    HB = B // 2
    HALF = N // 2
    STEPS = 2 * NT
    GROUPS = H * G
    ALLG = NCH * GROUPS
    ACC = 6
    PER = 2
    BANK = 512
    NB_ACC = NT // PER
    READS = NB_ACC // 2
    DVE_TILES = (
        (0,) * 2 + (1,) * 30,
        (1, 0, 0, 0) * 2 + (1, 0, 1) * 8,
        (1, 0, 0, 0) * 2 + (1, 0, 1) * 8,
        (1, 0, 0, 0) * 2 + (1,) * 24,
    )
    BY_MATMUL = (
        (0, 0, 1),
        (1, 0) * 4 + (0, 0, 1) * 8,
        (1, 0) * 4 + (0, 0, 1) * 8,
        (1, 0) * 4 + (0, 0, 0, 0, 1) * 5,
    )
    ACT_STORES = tuple(range(0, STEPS, 2))
    FIRST_BY_ACT = (0, 1, 2, 3)
    CONVERT_FROM, CONVERT_SPAN = 0, GROUPS - 6
    CONVERT_FROM_0, CONVERT_SPAN_0 = 10, GROUPS - 11
    DVE_STORE_LAG, ACT_STORE_LAG = 2, 4
    READ_AT, JOIN_AT = (1, 1), 2
    ADD_AT, MOMENTS_AT, NORMALIZE_AT = 3, 4, (6, 7)
    X_AT = 10
    SROW_AFTER = 6
    FIRST_CONVERT = (-1, 0, 1, 1, 2, 2, 3, 3)
    FIRST_TURN = (0, 0, 1, 1, 2, 2, 3, 3)
    FIRST_STORE = (0, 1, 2, 2, 3, 3, 4, 4)
    PROJ_CONVERT = {2: 1, 8: 2, 13: 3}
    PROJ_TURN = {4: 0, 9: 1, 14: 2}
    PROJ_STORE = {7: 0, 12: 1}
    SPLIT_AT = (None, 2, 4, 6)
    SPLIT_DVE_LAG, SPLIT_ACT_LAGS = 2, (3, 5, 6)
    BIG = float(2 ** 60)
    TINY = float(2.0 ** -100)
    EPS = 1e-5
    CSLOTS, ISLOTS, JSLOTS = 5, 3, 2
    EDGE, I_SHIFT = -0.125, 5
    XSUMS = N // BANK

    HALF_STEPS = NT
    convert_at, turn_at, store_at = {}, {}, {}
    for k in range(HALF_STEPS, STEPS):
        i = k - HALF_STEPS
        convert_at.setdefault(FIRST_CONVERT[i], []).append(k)
        turn_at.setdefault(FIRST_TURN[i], []).append(k)
        store_at.setdefault(FIRST_STORE[i], []).append(k)
    for k in range(STEPS, NCH * STEPS):
        c, i = k // STEPS, k % STEPS
        start, span = (CONVERT_FROM_0, CONVERT_SPAN_0) if c == 1 else (CONVERT_FROM, CONVERT_SPAN)
        at = (c - 1) * GROUPS + start + i * span // (STEPS - 1)
        convert_at.setdefault(at, []).append(k)
        turn_at.setdefault(at, []).append(k)
        needed = c * GROUPS + (0 if i < HALF_STEPS else G // 2)
        by = (at + ACT_STORE_LAG, needed + 1) if i in ACT_STORES else (at + DVE_STORE_LAG, needed - 1)
        store_at.setdefault(min(by), []).append(k)

    def dve_tiles(g):
        tiles = DVE_TILES[g // GROUPS]
        return tiles[g % len(tiles)]

    def j_by_matmul(g):
        which = BY_MATMUL[g // GROUPS]
        return bool(which[g % len(which)])

    def act_stores(k):
        return k in FIRST_BY_ACT or k >= STEPS and k % STEPS in ACT_STORES

    def stores_before(k, by_act):
        return sum(act_stores(i) == by_act for i in range(k))

    act_before, dve_before = [0], [0]
    j_groups = [g for g in range(ALLG) if not j_by_matmul(g)]
    j_before = [0]
    for g in range(ALLG):
        act_before.append(act_before[-1] + GT - dve_tiles(g))
        dve_before.append(dve_before[-1] + dve_tiles(g))
        j_before.append(j_before[-1] + (not j_by_matmul(g)))

    def bank_of(s, j):
        return ((s % H) * NB_ACC + j) % ACC

    def reads_before(s, j):
        had = [(s0, j0) for s0 in range(s) for j0 in range(NB_ACC) if bank_of(s0, j0) == bank_of(s, j)]
        return had[-1][0] * READS + had[-1][1] // 2 + 1 if had else None

    ctx = ExitStack()
    with ctx:
        def sb(name, shape, dt):
            return ctx.enter_context(nc.sbuf_tensor(name, shape, dt))

        def pb(name, shape, dt):
            return ctx.enter_context(nc.psum_tensor(name, shape, dt))

        def sem(name):
            return ctx.enter_context(nc.semaphore(name))

        adj_rows = sb("adj_rows", [P, 2, HALF], i32)
        edge_rows = sb("edge_rows", [P, 2, HALF], fp8)
        edges = sb("edges", [P, 2, G, GB * CH * R], u8)
        above = sb("above", [P, CSLOTS, GB * CH * R], u8)
        ij = sb("ij", [P, ISLOTS + JSLOTS, GB * CH * R], u8)
        imat, jmat = ij[:, 0:ISLOTS, :], ij[:, ISLOTS:, :]
        weights = sb("weights", [P, T + 1, H, 2 * KP], bf16)
        srow = sb("srow", [P, 2, CH], fp32)
        heads = sb("heads", [P, NT, H, K], fp32)
        joined = sb("joined", [P, NT, 2, K], fp32)
        y = sb("y", [P, NT, F], fp32)
        rden = sb("rden", [P, NT, H], fp32)
        stats = sb("stats", [P, NT, 6], fp32)
        moments = sb("moments", [P, NT, 2], fp32)
        rstd = sb("rstd", [P, NT], fp32)
        power = sb("power", [P, NT], fp32)
        ident = sb("ident", [P, P], fp32)
        ident16 = sb("ident16", [P, P], bf16)
        ones = sb("ones", [P, P], bf16)
        onesf = sb("onesf", [H, P], fp32)
        wraw = sb("wraw", [P, F], fp32)
        avec = sb("avec", [P, H, 2, D], fp32)
        wprod = sb("wprod", [P, H, 2, D], fp32)
        wa = sb("wa", [P, 2, H], fp32)
        wx = sb("wx", [P, H * K + H], fp32)
        xsum = sb("xsum", [P, XSUMS], fp32)
        t = sb("t", [P, T, H], fp32)
        tneg = sb("tneg", [P, T, H], fp32)
        tbig = sb("tbig", [P, T, H], fp32)
        eA = sb("eA", [P, T, H], fp32)
        eB = sb("eB", [P, T, H], fp32)
        ab = sb("ab", [P, T, H, 2], fp32)
        tmax = sb("tmax", [P, H], fp32)
        tcol = sb("tcol", [H, 1], fp32)
        tdiag = sb("tdiag", [H, H], fp32)
        tall = sb("tall", [P, H], fp32)
        meanw = sb("meanw", [P, H, K], fp32)
        split = sb("split", [P, T * K], fp32)
        s_all = sb("s_all", [P, H, T], fp32)
        s_turned = sb("s_turned", [H * T, P], fp32)

        early = edges[:, 1, :, :].rearrange("p g c -> p (g c)").bitcast(fp32)
        WIDE = H * K + H
        features = early[:, 0:T * WIDE].rearrange("p (t c) -> p t c", t=T)
        h1 = features[:, :, 0:H * K].rearrange("p t (h k) -> p t h k", h=H)
        unsplit = [early[:, T * WIDE + i * T * K:T * WIDE + (i + 1) * T * K] for i in range(3)] + [split[:, :]]
        xq = above[:, :, :].rearrange("p s c -> p (s c)").bitcast(fp32)[:, 0:T * F].rearrange(
            "p (b r f) -> p b r f", b=B, r=R)
        xT = ij[:, :, :].rearrange("p s c -> p (s c)").bitcast(fp32)[:, 0:T * F]

        def split_a(h):
            return unsplit[h % 2].rearrange("p (t k) -> p t k", k=K)

        def split_b(h):
            return unsplit[2 + h % 2].rearrange("p (t k) -> p t k", k=K)

        def part_of(h, side, part):
            return weights[:, 0:T, h, side * KP + part * K:side * KP + (part + 1) * K]

        acc_all = pb("acc_all", [P, ACC, PER, BANK // PER], fp32)
        acc = acc_all[:, :, :, 0:2 * KP]
        tr = [pb(f"tr{i}", [P, 2 * BANK], bf16) for i in range(2)]

        def columns(i, j):
            first = (i // R) * CH * R + i % R
            if j is None:
                return slice(first, first + CH * R - R + 1, R)
            return slice(first + j * P * R, first + (j + 1) * P * R - R + 1, R)

        def start_bank(u):
            return acc_all[:, u % ACC, :, :].rearrange("p j c -> p (j c)")

        U_XT = 0
        U_PROJ = U_XT + N // BANK
        U_S = U_PROJ + T // 2
        U_TMAX = U_S + 1
        U_TALL = U_TMAX + 1
        U_MEAN = U_TALL + 1
        U_ALL = U_MEAN + 1
        VECTOR_READS = tuple(range(U_PROJ + 1, U_S, 2)) + (U_TMAX, U_TALL, U_MEAN)

        x_in = [sem(f"x_in{i}") for i in range(2)]
        w_in, a_in, y_in = sem("w_in"), sem("a_in"), sem("y_in")
        adj_in = [sem(f"adj_in{i}") for i in range(2)]
        srow_in = [sem(f"srow_in{i}") for i in range(2)]
        s_out, y_out = sem("s_out"), sem("y_out")
        ident_ready, consts_ready = sem("ident_ready"), sem("consts_ready")
        pool_chain = sem("pool_chain")
        dve_chain = sem("dve_chain")
        wx_ready = sem("wx_ready")
        start_filled = sem("start_filled")
        start_read_act = sem("start_read_act")
        start_read_dve = sem("start_read_dve")
        s_ready = sem("s_ready")
        tmax_ready, tdiag_ready = sem("tmax_ready"), sem("tdiag_ready")
        t_ready = sem("t_ready")
        exp_in, exp_done = sem("exp_in"), sem("exp_done")
        a_residual1, a_residual2 = sem("a_residual1"), sem("a_residual2")
        b_product = sem("b_product")
        b_residual1, b_residual2 = sem("b_residual1"), sem("b_residual2")
        b_high = sem("b_high")
        a_middle, b_middle = sem("a_middle"), sem("b_middle")
        a_split, b_split = sem("a_split"), sem("b_split")
        mean_split = sem("mean_split")
        rows_converted = sem("rows_converted")
        words_turned = sem("words_turned")
        stored_act, stored_dve = sem("stored_act"), sem("stored_dve")
        act_above, dve_above = sem("act_above"), sem("dve_above")
        i_ready, j_ready = sem("i_ready"), sem("j_ready")
        group_summed = sem("group_summed")
        first_summed = sem("first_summed")
        sums_read = sem("sums_read")
        moments_ready, rstd_ready, y_normed = sem("moments_ready"), sem("rstd_ready"), sem("y_normed")

        def store_place(k):
            c, n, half = k // STEPS, k % NT, k // NT % 2
            blocks = edges[:, c % 2, :, :].rearrange("p g (b x) -> p (g b) x", b=GB)
            return blocks[:, half * HB:(half + 1) * HB, n * P * R:(n + 1) * P * R]

        def start_was_read(eng, u):
            by_dve = sum(v <= u for v in VECTOR_READS)
            if u in VECTOR_READS:
                eng.wait_ge(start_read_dve, by_dve)
            else:
                eng.wait_ge(start_read_act, u + 1 - by_dve)

        def heads_are_split(eng):
            eng.wait_ge(exp_in, 2)
            eng.wait_ge(a_split, H)
            eng.wait_ge(b_split, H)

        def was_stored(eng, k):
            eng.wait_ge(stored_act if act_stores(k) else stored_dve, stores_before(k + 1, act_stores(k)))

        block = ctx.enter_context(nc.Block())

        x_tiles = x.rearrange("(b q r) f -> q b (r f)", q=P, r=R)
        x_rows = x.rearrange("(c b q r) f -> c q b r f", c=NCH, q=P, r=R)
        out_rows = out.rearrange("(c b q r) f -> c q b r f", c=NCH, q=P, r=R)
        y_rows = y[:, :, :].rearrange("p (b r) f -> p b r f", r=R)
        adj_tiles = adj.rearrange("(b q r) m -> b r q m", q=P, r=R)

        @block.sync
        def _(sp):
            for i in range(2):
                sp.dma_start(xq[:, i * HB:(i + 1) * HB, :, :].rearrange("p b r f -> p b (r f)"),
                             x_tiles[:, i * HB:(i + 1) * HB, :]).then_inc(x_in[i], 16)
            sp.dma_start(wraw[:, :], W).then_inc(w_in, 16)
            sp.dma_start(avec[:, :, :, :].rearrange("p h k d -> p (h k d)"),
                         a.rearrange("h e o -> (h e o)").partition_broadcast(P)).then_inc(a_in, 16)

            def load_adj(k):
                if k >= 2:
                    sp.wait_ge(rows_converted, k - 1)
                n, half = k // STEPS * NT + k % NT, k // NT % 2
                sp.dma_start(adj_rows[:, k % 2, :],
                             adj_tiles[n // R, n % R, :, half * HALF:(half + 1) * HALF]).then_inc(adj_in[k % 2], 16)

            def load_srow(s):
                c, h = s // H, s % H
                if s >= 2:
                    sp.wait_ge(act_above, act_before[(s - 1) * G])
                    sp.wait_ge(dve_above, dve_before[(s - 1) * G])
                sp.dma_start(srow[:, s % 2, :],
                             score_rows[h, c * CH:(c + 1) * CH].partition_broadcast(P)).then_inc(srow_in[s % 2], 16)

            for k in range(SROW_AFTER):
                load_adj(k)
            sp.wait_ge(s_out, 16)
            load_srow(0)
            for k in range(SROW_AFTER, HALF_STEPS + len(convert_at[-1]) + 2):
                load_adj(k)
            load_srow(1)
            sp.dma_start(y_rows, x_rows[0]).then_inc(y_in, 16)
            for g in range(ALLG):
                c, gc, s = g // GROUPS, g % GROUPS, g // G
                if g % G == 0 and s >= 1 and s + 1 < NCH * H:
                    load_srow(s + 1)
                for k in convert_at.get(g, ()):
                    if k + 2 < NCH * STEPS:
                        load_adj(k + 2)
                if gc == X_AT and c:
                    sp.wait_ge(y_normed, c)
                    sp.dma_start(out_rows[c - 1], y_rows).then_inc(y_out, 16)
                    sp.wait_ge(y_out, 16 * c)
                    sp.dma_start(y_rows, x_rows[c]).then_inc(y_in, 16)
            for i in range(READS):
                some = slice(i * NT // R // READS, (i + 1) * NT // R // READS)
                sp.wait_ge(y_normed, NCH + i)
                sp.dma_start(out_rows[NCH - 1][:, some, :, :], y_rows[:, some, :, :]).then_inc(y_out, 16)
            sp.wait_ge(y_out, 16 * (NCH - 1 + READS))

        @block.gpsimd
        def _(pool):
            made = [0]

            def link(ins):
                made[0] += 1
                ins.then_inc(pool_chain, 1)
                pool.wait_ge(pool_chain, made[0])

            link(pool.memset(ident[:, :], 0.0))
            pool.affine_select(out=ident[:, :], in_=ident[:, :], compare_op=ALU.not_equal, fill=1.0,
                               base=0, pattern=[[-1, P]], channel_multiplier=1).then_inc(ident_ready, 1)
            pool.wait_ge(ident_ready, 1)
            link(pool.tensor_copy(ident16[:, :], ident[:, :]))
            link(pool.memset(ones[:, :], 1.0))
            link(pool.memset(power[:, :], -0.5))
            link(pool.memset(meanw[:, :, :], 0.0))
            pool.memset(onesf[:, :], 1.0).then_inc(consts_ready, 1)

            pool.wait_ge(exp_done, 2)
            link(pool.tensor_scalar(eB[:, :, :], eB[:, :, :], -1.0, 0.0, ALU.mult, ALU.add))
            for h in range(H):
                if h >= 2:
                    pool.wait_ge(b_split, h - 1)
                pool.tensor_tensor(split_b(h), h1[:, :, h, :],
                                   eB[:, :, h:h + 1].broadcast_to([P, T, K]), ALU.mult).then_inc(b_product, 1)
                for part in range(2):
                    pool.wait_ge((b_high, b_middle)[part], h + 1)
                    pool.tensor_tensor(split_b(h), split_b(h), part_of(h, 1, part),
                                       ALU.subtract).then_inc((b_residual1, b_residual2)[part], 1)

            for times in range(NCH - 1 + READS):
                part = max(times - (NCH - 1), 0)
                rows = slice(0, NT) if times < NCH - 1 else slice(part * NT // READS, (part + 1) * NT // READS)
                pool.wait_ge(moments_ready, times + 1)
                link(pool.tensor_scalar(rstd[:, rows], moments[:, rows, 1], 1.0, EPS, ALU.mult, ALU.add))
                pool.tensor_tensor(rstd[:, rows], rstd[:, rows], power[:, rows], ALU.pow).then_inc(rstd_ready, 1)

        @block.scalar
        def _(act):
            def store_edges(k):
                act.wait_ge(words_turned, k + 1)
                c = k // STEPS
                if c == 1:
                    heads_are_split(act)
                if c >= 2:
                    act.wait_ge(group_summed, (c - 1) * GROUPS)
                act.copy(store_place(k).bitcast(fp32), tr[k % 2][:, :].bitcast(fp32).rearrange("p (b n) -> p b n", b=HB)
                         ).then_inc(stored_act, 1)

            for k in range(N // BANK):
                act.wait_ge(start_filled, U_XT + k + 1)
                nc.scalar.activation(xT[:, k * BANK:(k + 1) * BANK], start_bank(U_XT + k), ACT.Identity,
                                     accum_out=xsum[:, k:k + 1]).then_inc(start_read_act, 1)
            for p in range(T // 2):
                if p % 2 == 0:
                    act.wait_ge(start_filled, U_PROJ + p + 1)
                    act.copy(features[:, 2 * p:2 * p + 2, :].rearrange("p t c -> p (t c)"),
                             start_bank(U_PROJ + p)[:, 0:2 * WIDE]).then_inc(start_read_act, 1)
                if p in PROJ_STORE:
                    store_edges(PROJ_STORE[p])
            act.wait_ge(start_filled, U_S + 1)
            act.copy(s_turned[:, :], start_bank(U_S)[:, 0:P]).then_inc(start_read_act, 1)
            start_was_read(act, U_S)
            act.dma_start(score_rows.rearrange("h (t q) -> (h t) q", q=P), s_turned[:, :]).then_inc(s_out, 16)
            for k in range(len(PROJ_STORE), 4):
                store_edges(k)
            act.wait_ge(exp_in, 1)
            nc.scalar.activation(eA[:, :, :], eA[:, :, :], ACT.Exp).then_inc(exp_done, 1)
            nc.scalar.activation(eB[:, :, :], eB[:, :, :], ACT.Exp, scale=0.01).then_inc(exp_done, 1)
            act.wait_ge(exp_in, 2)
            nc.scalar.activation(ab[:, :, :, :], ab[:, :, :, :], ACT.Exp).then_inc(exp_done, 1)

            def round_a(h, part):
                act.wait_ge((a_residual1, a_residual2)[part - 1], h + 1)
                act.copy(part_of(h, 0, part), split_a(h)).then_inc((a_middle, a_split)[part - 1], 1)

            def round_b(h, part):
                act.wait_ge((b_product, b_residual1, b_residual2)[part], h + 1)
                act.copy(part_of(h, 1, part), split_b(h)).then_inc((b_high, b_middle, b_split)[part], 1)

            def compare(g, tiles):
                h, b, s = g // G % H, g % G, g // G
                for i in tiles:
                    nc.scalar.activation(above[:, g % CSLOTS, columns(i, None)], srow[:, s % 2, :], ACT.Sigmoid,
                                         bias=tbig[:, b * GT + i, h:h + 1], scale=BIG).then_inc(act_above, 1)

            round_b(0, 0)
            round_a(0, 1)
            act.wait_ge(t_ready, 1)
            act.wait_ge(srow_in[0], 16)
            mine = [(g, i) for g in range(2) for i in range(GT - dve_tiles(g))]
            rounds = [(round_b, 1), (round_a, 2), (round_b, 2)]
            for at, (g, i) in enumerate(mine):
                compare(g, (i,))
                if at < len(rounds):
                    rounds[at][0](0, rounds[at][1])
            for g in range(ALLG):
                s = g // G
                if g >= 2:
                    if g % G == 0:
                        act.wait_ge(srow_in[s % 2], 16 * (s // 2 + 1))
                    if g >= CSLOTS:
                        act.wait_ge(i_ready, g - CSLOTS + 1)
                    compare(g, range(GT - dve_tiles(g)))
                for k in store_at.get(g, ()):
                    if act_stores(k):
                        store_edges(k)
                for hs in range(1, H):
                    for part in range(PARTS):
                        if g == SPLIT_AT[hs] + SPLIT_ACT_LAGS[part]:
                            round_b(hs, part)
                            if part < PARTS - 1:
                                round_a(hs, part + 1)

        @block.vector
        def _(dve):
            made = [0]

            def link(ins):
                made[0] += 1
                ins.then_inc(dve_chain, 1)
                dve.wait_ge(dve_chain, made[0])

            def convert(k):
                dve.wait_ge(adj_in[k % 2], 16 * (k // 2 + 1))
                if k >= 2:
                    dve.wait_ge(words_turned, k - 1)
                nc.vector.tensor_scalar(edge_rows[:, k % 2, :], adj_rows[:, k % 2, :], 0.0, EDGE,
                                        ALU.is_gt, ALU.mult, saturate=False).then_inc(rows_converted, 1)

            def store_edges(k):
                dve.wait_ge(words_turned, k + 1)
                c = k // STEPS
                if c == 1:
                    heads_are_split(dve)
                if c >= 2:
                    dve.wait_ge(group_summed, (c - 1) * GROUPS)
                nc.vector.tensor_copy(store_place(k).bitcast(u32), tr[k % 2][:, :].bitcast(u32).rearrange("p (b n) -> p b n", b=HB)
                                      ).then_inc(stored_dve, 1)

            dve.wait_ge(w_in, 16)
            dve.wait_ge(a_in, 16)
            w3 = wraw[:, :].rearrange("p (h d) -> p h d", h=H)
            link(nc.vector.tensor_tensor(wprod[:, :, :, :], w3.unsqueeze(2).broadcast_to([P, H, 2, D]),
                                         avec[:, :, :, :], ALU.mult))
            link(nc.vector.tensor_reduce(wa[:, :, :].rearrange("p k h -> p h k"), wprod[:, :, :, :], AX.X, ALU.add))
            by_head = wx[:, 0:H * K].rearrange("p (h k) -> p h k", h=H)
            nc.vector.tensor_copy(by_head[:, :, 0:D], w3)
            nc.vector.tensor_copy(by_head[:, :, D], wa[:, 1, :])
            nc.vector.tensor_copy(wx[:, H * K:], wa[:, 0, :]).then_inc(wx_ready, 1)
            convert(0)
            for p in range(T // 2):
                if p % 2:
                    dve.wait_ge(start_filled, U_PROJ + p + 1)
                    nc.vector.tensor_copy(features[:, 2 * p:2 * p + 2, :].rearrange("p t c -> p (t c)"),
                                          start_bank(U_PROJ + p)[:, 0:2 * WIDE]).then_inc(start_read_dve, 1)
                if p in PROJ_CONVERT:
                    convert(PROJ_CONVERT[p])

            start_was_read(dve, U_S - 2)
            start_was_read(dve, U_S - 1)
            nc.vector.tensor_copy(s_all[:, :, :].rearrange("p h t -> p t h"),
                                  features[:, :, H * K:]).then_inc(s_ready, 1)
            link(nc.vector.tensor_copy(t[:, :, :], h1[:, :, :, D]))
            nc.vector.tensor_reduce(tmax[:, :], t[:, :, :].rearrange("p t h -> p h t"), AX.X,
                                    ALU.max).then_inc(tmax_ready, 1)
            nc.vector.memset(h1[:, :, :, D], 1.0)
            dve.wait_ge(start_filled, U_TMAX + 1)
            link(nc.vector.tensor_reduce(tcol[:, :], start_bank(U_TMAX)[0:H, 0:P], AX.X, ALU.max))
            nc.vector.tensor_scalar(tdiag[:, :], ident[0:H, 0:H], tcol[:, :], None,
                                    ALU.mult).then_inc(tdiag_ready, 1)
            dve.sem_inc(start_read_dve, 1)
            dve.wait_ge(start_filled, U_TALL + 1)
            nc.vector.tensor_copy(tall[:, :], start_bank(U_TALL)[:, 0:H]).then_inc(start_read_dve, 1)
            start_was_read(dve, U_TALL)
            for to in (eA, eB):
                last = nc.vector.tensor_tensor(to[:, :, :], t[:, :, :],
                                               tall[:, :].unsqueeze(1).broadcast_to([P, T, H]), ALU.subtract)
            last.then_inc(exp_in, 1)
            nc.vector.tensor_scalar(tneg[:, :, :], t[:, :, :], -1.0, None, ALU.mult)
            nc.vector.tensor_scalar(tbig[:, :, :], t[:, :, :], BIG, None, ALU.mult).then_inc(t_ready, 1)
            dve.wait_ge(start_filled, U_S + 1)
            s_th = s_all[:, :, :].rearrange("p h t -> p t h")
            link(nc.vector.tensor_tensor(s_th, s_th, tall[:, :].unsqueeze(1).broadcast_to([P, T, H]),
                                         ALU.add))
            nc.vector.tensor_scalar(ab[:, :, :, 0], s_th, 0.99, 0.0, ALU.mult, ALU.min)
            nc.vector.tensor_scalar(ab[:, :, :, 1], s_th, -0.99, 0.0, ALU.mult,
                                    ALU.min).then_inc(exp_in, 1)

            def compare(g):
                h, b, s = g // G % H, g % G, g // G
                n = dve_tiles(g)
                if n and b < 2:
                    dve.wait_ge(srow_in[s % 2], 16 * (s // 2 + 1))
                if n and g >= CSLOTS:
                    dve.wait_ge(i_ready, g - CSLOTS + 1)
                for i in range(GT - n, GT):
                    nc.vector.tensor_scalar(above[:, g % CSLOTS, columns(i, None)], srow[:, s % 2, :],
                                            tneg[:, b * GT + i, h:h + 1], None, ALU.is_ge).then_inc(dve_above, 1)

            def split_head(h, part):
                if part == 0:
                    if h >= 2:
                        dve.wait_ge(a_split, h - 1)
                    link(nc.vector.tensor_tensor(split_a(h), h1[:, :, h, :],
                                                 eA[:, :, h:h + 1].broadcast_to([P, T, K]), ALU.mult))
                    link(nc.vector.tensor_copy(part_of(h, 0, 0), split_a(h)))
                else:
                    dve.wait_ge(a_middle, h + 1)
                nc.vector.tensor_tensor(split_a(h), split_a(h), part_of(h, 0, part),
                                        ALU.subtract).then_inc((a_residual1, a_residual2)[part], 1)

            convert(4)
            convert(5)
            dve.wait_ge(exp_done, 1)
            split_head(0, 0)
            store_edges(4)
            convert(6)
            split_head(0, 1)
            store_edges(5)
            convert(7)
            dve.wait_ge(consts_ready, 1)
            dve.wait_ge(start_filled, U_MEAN + 1)
            link(nc.vector.tensor_scalar(meanw[0:XSUMS, :, :].rearrange("p h k -> p (h k)"),
                                         start_bank(U_MEAN)[0:XSUMS, 0:H * K], TINY, None,
                                         ALU.mult))
            dve.sem_inc(start_read_dve, 1)
            link(nc.vector.memset(meanw[0:XSUMS, :, D], TINY * (N // XSUMS)))
            both = weights[:, T, :, :].rearrange("p h (z c k) -> p h z c k", z=2, k=K)
            for part in range(PARTS):
                link(nc.vector.tensor_copy(both[:, :, :, part, :], meanw[:, :, :].unsqueeze(2).broadcast_to([P, H, 2, K])))
                if part < PARTS - 1:
                    link(nc.vector.tensor_tensor(meanw[:, :, :], meanw[:, :, :], both[:, :, 0, part, :], ALU.subtract))
            nc.vector.sem_inc(mean_split, 1)
            compare(0)
            store_edges(6)
            for k in convert_at[-1]:
                convert(k)
            store_edges(7)

            def make_i(g):
                c, b = g // GROUPS, g % G
                dve.wait_ge(act_above, act_before[g + 1])
                dve.wait_ge(dve_above, dve_before[g + 1])
                if g % GROUPS in (0, G // 2):
                    steps = STEPS * c + (HALF_STEPS if g % GROUPS == 0 else STEPS)
                    dve.wait_ge(stored_act, stores_before(steps, True))
                    if stores_before(steps, False):
                        dve.wait_ge(stored_dve, stores_before(steps, False))
                if g == 0:
                    dve.wait_ge(start_filled, U_ALL)
                if g >= ISLOTS:
                    dve.wait_ge(group_summed, g - ISLOTS + 1)
                nc.vector.scalar_tensor_tensor(imat[:, g % ISLOTS, :].bitcast(u32),
                                               above[:, g % CSLOTS, :].bitcast(u32), I_SHIFT,
                                               edges[:, c % 2, b, :].bitcast(u32), ALU.logical_shift_left,
                                               ALU.bitwise_and).then_inc(i_ready, 1)

            def make_j(g):
                c, b = g // GROUPS, g % G
                n = j_before[g]
                dve.wait_ge(i_ready, g + 1)
                if n >= JSLOTS:
                    dve.wait_ge(group_summed, j_groups[n - JSLOTS] + 1)
                nc.vector.tensor_tensor(jmat[:, n % JSLOTS, :].bitcast(u32), imat[:, g % ISLOTS, :].bitcast(u32),
                                        edges[:, c % 2, b, :].bitcast(u32), ALU.bitwise_xor).then_inc(j_ready, 1)

            def read_sums(s, i):
                if i < READS - 1:
                    dve.wait_ge(first_summed, s * (READS - 1) + i + 1)
                else:
                    dve.wait_ge(group_summed, (s + 1) * G)
                first = bank_of(s, 2 * i)
                view = acc[:, first:first + 2, :, :].rearrange("p b j (z c k) -> p (b j) z k c", z=2, k=K)
                nc.vector.tensor_reduce(joined[:, i * NT // READS:(i + 1) * NT // READS, :, :], view, AX.X,
                                        ALU.add).then_inc(sums_read, 1)

            def join(s, first=0, end=NT):
                c, h = s // H, s % H
                dve.wait_ge(sums_read, s * READS + end * READS // NT)
                if s == 0:
                    dve.wait_ge(exp_done, 3)
                rows = ab[:, c * NT + first:c * NT + end, h, :]
                sides = joined[:, first:end, :, :]
                link(nc.vector.tensor_tensor(sides, sides, rows.unsqueeze(3).broadcast_to([P, end - first, 2, K]),
                                             ALU.mult))
                link(nc.vector.tensor_tensor(heads[:, first:end, h, :], sides[:, :, 0, :], sides[:, :, 1, :],
                                             ALU.add))

            def add_heads(c, h0=0, h1=H, first=0, end=NT):
                some = heads[:, first:end, h0:h1, 0:D]
                inverse = rden[:, first:end, h0:h1]
                link(nc.vector.reciprocal(inverse, heads[:, first:end, h0:h1, D]))
                link(nc.vector.tensor_tensor(some, some, inverse.unsqueeze(3).broadcast_to(
                    [P, end - first, h1 - h0, D]), ALU.mult))
                dve.wait_ge(y_in, 16 * (c + 1))
                y4 = y[:, first:end, :].rearrange("p j (h d) -> p j h d", h=H)[:, :, h0:h1, :]
                link(nc.vector.tensor_tensor(y4, y4, some, ALU.add))

            def take_moments(first=0, end=NT):
                for j in range(first, end):
                    last = nc.vector.bn_stats(stats[:, j, :], y[:, j, :])
                link(last)
                for j in range(first, end):
                    last = nc.vector.bn_aggr(moments[:, j, :], stats[:, j, :])
                last.then_inc(moments_ready, 1)

            def normalize(times, first, end):
                dve.wait_ge(rstd_ready, times)
                for j in range(first, end):
                    last = nc.vector.tensor_scalar(y[:, j, :], y[:, j, :], moments[:, j, 0:1], rstd[:, j:j + 1],
                                                   ALU.subtract, ALU.mult)
                return last

            for g in range(ALLG):
                c, gc, b, s = g // GROUPS, g % GROUPS, g % G, g // G
                if g + 1 < ALLG:
                    compare(g + 1)
                for k in store_at.get(g, ()):
                    if not act_stores(k):
                        store_edges(k)
                make_i(g)
                for k in convert_at.get(g, ()):
                    convert(k)
                for hs in range(1, H):
                    for part in range(PARTS - 1):
                        if g == SPLIT_AT[hs] + part * SPLIT_DVE_LAG:
                            split_head(hs, part)
                for i in range(READS if s else 0):
                    if b == READ_AT[i]:
                        read_sums(s - 1, i)
                if b == JOIN_AT and s:
                    join(s - 1)
                if not j_by_matmul(g):
                    make_j(g)
                if c and gc == ADD_AT:
                    add_heads(c - 1)
                if c and gc == MOMENTS_AT:
                    take_moments()
                for half, at in enumerate(NORMALIZE_AT):
                    if c and gc == at:
                        last = normalize(c, half * NT // 2, (half + 1) * NT // 2)
                        if half:
                            last.then_inc(y_normed, 1)
                if g == ALLG - 2:
                    add_heads(NCH - 1, 0, H - 1)
            for i in range(READS):
                rows = i * NT // READS, (i + 1) * NT // READS
                read_sums(NCH * H - 1, i)
                join(NCH * H - 1, *rows)
                add_heads(NCH - 1, H - 1, H, *rows)
                take_moments(*rows)
            for i in range(READS):
                normalize(NCH + i, i * NT // READS, (i + 1) * NT // READS).then_inc(y_normed, 1)

        @block.tensor
        def _(pe):
            def turn_words(k):
                pe.wait_ge(rows_converted, k + 1)
                if k >= 2:
                    was_stored(pe, k - 2)
                for b in range(HB):
                    last = nc.tensor.transpose(tr[k % 2][:, b * P:(b + 1) * P],
                                               edge_rows[:, k % 2, b * P * R:(b + 1) * P * R].bitcast(bf16),
                                               ident16[:, :])
                last.then_inc(words_turned, 1)

            def free_bank(u):
                if u >= ACC:
                    start_was_read(pe, u - ACC)
                return start_bank(u)

            pe.wait_ge(ident_ready, 1)
            for k in range(N // BANK):
                pe.wait_ge(x_in[2 * k // (N // BANK)], 16)
                to = free_bank(U_XT + k)
                for i in range(GT):
                    last = nc.tensor.transpose(to[:, i * P:(i + 1) * P], xq[:, k * GB + i // R, i % R, :], ident[:, :])
                last.then_inc(start_filled, 1)
            pe.wait_ge(wx_ready, 1)
            pe.wait_ge(consts_ready, 1)
            for p in range(T // 2):
                if p in PROJ_TURN:
                    turn_words(PROJ_TURN[p])
                to = free_bank(U_PROJ + p)
                start_was_read(pe, U_XT + p // 2)
                for z in range(2):
                    k = 2 * p + z
                    last = nc.tensor.matmul(to[:, z * WIDE:(z + 1) * WIDE], xT[:, k * P:(k + 1) * P], wx[:, :],
                                            start=True, stop=True)
                last.then_inc(start_filled, 1)
            to = free_bank(U_S)
            pe.wait_ge(s_ready, 1)
            nc.tensor.transpose(to[:, 0:P], s_all[:, :, :].rearrange("p h t -> p (h t)"),
                                ident[:, :]).then_inc(start_filled, 1)
            to = free_bank(U_TMAX)
            pe.wait_ge(tmax_ready, 1)
            nc.tensor.transpose(to[0:H, 0:P], tmax[:, :], ident[:, :]).then_inc(start_filled, 1)
            to = free_bank(U_TALL)
            pe.wait_ge(tdiag_ready, 1)
            nc.tensor.matmul(to[:, 0:H], onesf[:, :], tdiag[:, :], start=True, stop=True).then_inc(start_filled, 1)
            nc.tensor.matmul(free_bank(U_MEAN)[0:XSUMS, 0:H * K], xsum[:, :],
                             wx[:, 0:H * K], start=True, stop=True).then_inc(start_filled, 1)
            for k in range(len(PROJ_TURN), HALF_STEPS):
                turn_words(k)
            for u in range(U_ALL - ACC, U_ALL):
                start_was_read(pe, u)

            for g in range(ALLG):
                c, gc, h, b, s = g // GROUPS, g % GROUPS, g // G % H, g % G, g // G
                for k in turn_at.get(g, ()):
                    turn_words(k)
                if b == 0 and c == 0:
                    if h == 0:
                        pe.wait_ge(mean_split, 1)
                    pe.wait_ge(a_split, h + 1)
                    pe.wait_ge(b_split, h + 1)
                pe.wait_ge(i_ready, g + 1)
                if not j_by_matmul(g):
                    pe.wait_ge(j_ready, j_before[g + 1])
                for j in range(NT):
                    bank = bank_of(s, j // PER)
                    if b == 0 and j % PER == 0:
                        had = reads_before(s, j // PER)
                        if had:
                            pe.wait_ge(sums_read, had)
                        nc.tensor.matmul(acc[:, bank, :, :], ones[:, :],
                                         weights[:, T, h, :].unsqueeze(1).broadcast_to([P, PER, 2 * KP]),
                                         start=True, stop=False, skip_group_check=True)
                    to = acc[:, bank, j % PER, :]
                    for i in range(GT):
                        k = b * GT + i
                        cols = columns(i, j)
                        i_m = imat[:, g % ISLOTS, cols].bitcast(fp8)
                        if j_by_matmul(g):
                            nc.tensor.matmul(to, i_m, weights[:, k, h, :], start=False, stop=False,
                                             skip_group_check=True)
                            j_m = edges[:, c % 2, b, cols].bitcast(fp8)
                        else:
                            nc.tensor.matmul(to[:, 0:KP], i_m, weights[:, k, h, 0:KP], start=False, stop=False,
                                             skip_group_check=True)
                            j_m = jmat[:, j_before[g] % JSLOTS, cols].bitcast(fp8)
                        last = nc.tensor.matmul(to[:, KP:2 * KP], j_m, weights[:, k, h, KP:2 * KP], start=False,
                                                stop=(b == G - 1 and i == GT - 1), skip_group_check=True)
                    if b == G - 1 and (j + 1) % (NT // READS) == 0 and j < NT - 1:
                        last.then_inc(first_summed, 1)
                last.then_inc(group_summed, 1)


def kernel(x, adj, L0_gnn_W, L0_gnn_a):
    import numpy as np
    import concourse.bacc as bacc
    from concourse.bass_utils import run_bass_kernel_spmd

    nc = bacc.Bacc("TRN2", target_bir_lowering=False, num_devices=1)
    arrays = {"x": x, "adj": adj, "W": L0_gnn_W, "a": L0_gnn_a}
    arrays = {name: np.ascontiguousarray(value) for name, value in arrays.items()}
    args = [nc.dram_tensor(name, v.shape, mybir.dt.from_np(v.dtype), kind="ExternalInput").ap()
            for name, v in arrays.items()]
    heads = arrays["a"].shape[0]
    rows, features = arrays["x"].shape
    score_rows = nc.dram_tensor("score_rows", (heads, rows), mybir.dt.float32, kind="Internal").ap()
    out = nc.dram_tensor("out", (rows, features), mybir.dt.float32, kind="ExternalOutput").ap()
    graph_attention_residual_norm(nc, *args, score_rows, out)
    r = run_bass_kernel_spmd(nc, [arrays], core_ids=[0])
    return r.results[0]["out"]
```
